# Optimizing a Trainium2 kernel written in Bass

```python
import numpy as np
import jax
import jax.numpy as jnp

def _softmax(x, axis=-1):
    return jax.nn.softmax(x, axis=axis)

def _gelu(x):
    return jax.nn.gelu(x, approximate=True)

def _silu(x):
    return jax.nn.silu(x)

def _sigmoid(x):
    return jax.nn.sigmoid(x)

def _layernorm(x, axis=-1, eps=1e-05):
    m = jnp.mean(x, axis=axis, keepdims=True)
    v = jnp.var(x, axis=axis, keepdims=True)
    return (x - m) / jnp.sqrt(v + eps)

def _scatter_add(tgt, idx, src, axis=0):
    return tgt.at[idx].add(src)

def _segment_sum(src, seg, n):
    return jax.ops.segment_sum(src, seg, n)
kernel_name = 'mk_adj_preln_d1_adj_r2_8236ef'

def setup_inputs(seed: int=0):
    np.random.seed(seed)
    _w = jnp.asarray

    def _rec_inputs():
        import jax
        import jax.numpy as jnp
        _gk = jax.random.key(seed)
        x = 7.22e-05 + 1 * jax.random.normal(jax.random.fold_in(_gk, 1), (16, 512, 512), jnp.float32)
        _w = (1.0 + jnp.arange(512, dtype=jnp.float32)) ** (-0.5)
        _w = _w / _w.mean()
        _pij = jnp.clip(0.015625 * _w[:, None] * _w[None, :], 0.0, 1.0)
        _a = jax.random.uniform(jax.random.fold_in(_gk, 2), (16, 512, 512)) < _pij
        _a = jnp.logical_or(_a, jnp.eye(512, dtype=bool))
        adj = _a.astype(jnp.int32)
        return (x, adj)
    x, adj = _rec_inputs()

    def _L0_gnn_setup():
        import jax, jax.numpy as jnp
        import numpy as np
        import math
        D_MODEL = 512
        N_HEADS = 16
        D_HEAD = D_MODEL // N_HEADS
        B, S = (4, 1024)
        key = jax.random.key(seed)
        ks = jax.random.split(key, 10)
        x = jax.random.normal(ks[0], (B, S, D_MODEL), dtype=jnp.float32)
        mask = jax.random.randint(ks[1], (B, S, S), 0, 2, dtype=jnp.int32)
        eye = jnp.eye(S, dtype=jnp.int32)[None]
        mask = jnp.maximum(mask, eye)
        std = 1.0 / math.sqrt(D_MODEL)
        Wq = jax.random.normal(ks[2], (D_MODEL, D_MODEL), dtype=jnp.float32) * std
        Wk = jax.random.normal(ks[3], (D_MODEL, D_MODEL), dtype=jnp.float32) * std
        Wv = jax.random.normal(ks[4], (D_MODEL, D_MODEL), dtype=jnp.float32) * std
        Wo = jax.random.normal(ks[5], (D_MODEL, D_MODEL), dtype=jnp.float32) * std
        bq = jnp.zeros((D_MODEL,), dtype=jnp.float32)
        bk = jnp.zeros((D_MODEL,), dtype=jnp.float32)
        bv = jnp.zeros((D_MODEL,), dtype=jnp.float32)
        bo = jnp.zeros((D_MODEL,), dtype=jnp.float32)
        return {'x': x, 'mask': mask, 'Wq': Wq, 'bq': bq, 'Wk': Wk, 'bk': bk, 'Wv': Wv, 'bv': bv, 'Wo': Wo, 'bo': bo}
    _L0_gnn_all = _L0_gnn_setup()
    _L0_gnn_in = {k: v for k, v in _L0_gnn_all.items() if k in ('Wq', 'bq', 'Wk', 'bk', 'Wv', 'bv', 'Wo', 'bo')}
    del _L0_gnn_all
    return {'x': x, 'adj': adj, 'L0_gnn_Wq': _L0_gnn_in['Wq'], 'L0_gnn_bq': _L0_gnn_in['bq'], 'L0_gnn_Wk': _L0_gnn_in['Wk'], 'L0_gnn_bk': _L0_gnn_in['bk'], 'L0_gnn_Wv': _L0_gnn_in['Wv'], 'L0_gnn_bv': _L0_gnn_in['bv'], 'L0_gnn_Wo': _L0_gnn_in['Wo'], 'L0_gnn_bo': _L0_gnn_in['bo']}

def reference(x, adj, L0_gnn_Wq, L0_gnn_bq, L0_gnn_Wk, L0_gnn_bk, L0_gnn_Wv, L0_gnn_bv, L0_gnn_Wo, L0_gnn_bo):
    import jax
    import jax.numpy as jnp

    def _L0_gnn_ref(x, mask, Wq, bq, Wk, bk, Wv, bv, Wo, bo):
        import jax, jax.numpy as jnp
        import numpy as np
        import math
        D_MODEL = 512
        N_HEADS = 16
        D_HEAD = D_MODEL // N_HEADS
        B, S = (4, 1024)
        b, s, _ = x.shape
        scale = 1.0 / math.sqrt(D_HEAD)

        def heads(t):
            return t.reshape(b, s, N_HEADS, D_HEAD).transpose(0, 2, 1, 3)
        q = heads(x @ Wq + bq)
        k = heads(x @ Wk + bk)
        v = heads(x @ Wv + bv)
        scores = jnp.einsum('bhqd,bhkd->bhqk', q, k) * scale
        scores = jnp.where(mask[:, None] == 0, -jnp.inf, scores)
        attn = jax.nn.softmax(scores, axis=-1)
        out = jnp.einsum('bhqk,bhkd->bhqd', attn, v)
        out = out.transpose(0, 2, 1, 3).reshape(b, s, D_MODEL)
        return out @ Wo + bo
    h = jnp.maximum(_layernorm(x, axis=-1), 0.0)
    x = x + _L0_gnn_ref(h, adj, L0_gnn_Wq, L0_gnn_bq, L0_gnn_Wk, L0_gnn_bk, L0_gnn_Wv, L0_gnn_bv, L0_gnn_Wo, L0_gnn_bo)
    return x

_drawn_inputs = setup_inputs


def setup_inputs(seed=0):
    import zlib

    import numpy as np

    out = dict(_drawn_inputs(seed))
    spreads = {'L0_gnn_bq': (0.0, 0.717),
     'L0_gnn_bk': (0.0, 0.8),
     'L0_gnn_bv': (0.0, 0.1),
     'L0_gnn_bo': (0.0, 0.1)}
    factors = {}
    for name, (base, spread) in spreads.items():
        noise = np.random.default_rng([zlib.crc32(name.encode()), seed]).standard_normal(out[name].shape)
        drawn = base * np.exp(spread * noise) if base else spread * noise
        out[name] = jnp.asarray(drawn.astype(out[name].dtype))
    for name, factor in factors.items():
        out[name] = (out[name] * factor).astype(out[name].dtype)
    return out
```

```python
from contextlib import ExitStack

import concourse.bass as bass
from concourse import mybir

ALU = mybir.AluOpType
ACT = mybir.ActivationFunctionType
F32 = mybir.dt.float32
F32R = mybir.dt.float32r
BF16 = mybir.dt.bfloat16
I32 = mybir.dt.int32

P = 128
HEADS = 16
DH = 32
HG = P // DH
STACK_SLOTS = 3
MASKED = -(2.0 ** 100)
MASKED_EXP = 2.0
NEG_MAX = -3.0e38
EPS = 1e-5
DMA = 16

WORK = {(g, s): [] for g in range(4) for s in range(4)}
for _g in range(4):
    WORK[_g, 0] += ["q"]
    WORK[_g, 1] += ["k"]
    WORK[_g, 3] += ["m"]
for _s in range(4):
    WORK[0, _s] += ["v"]
    WORK[3, _s] += ["b"]
WORK[1, 2] += ["h", "h"]
WORK[1, 3] += ["h", "h"]
for _s in range(4):
    WORK[1, _s] += ["o"]
PROLOGUE = list("hhhhqkqkbbbmb")
MAX_SHARE = [5, 6, 5, 0]
MAX_FIRST = [0, 5, 11, 16]


def batch_work(first, last):
    items, seen = [], {}
    for g in range(4):
        for s in range(4):
            for kind in WORK[g, s]:
                if first and kind == "o":
                    continue
                if last and (kind in "hb" or (kind in "qk" and g >= 2) or (kind == "m" and g == 3)):
                    continue
                items.append((g, s, kind, seen.get(kind, 0)))
                seen[kind] = seen.get(kind, 0) + 1
    return items


def build_kernel(nc, x, adj, Wq, bq, Wk, bk, Wv, bv, Wo, bo, out):
    B, S, D = x.shape
    T = S // P
    C = D // P
    G = HEADS // HG
    assert T == 4 and C == 4 and G == 4 and D == HEADS * DH and (B - 4) % 3 == 0
    TURNS = (B - 4) // 3
    SCALE = float(DH) ** -0.5
    MAXIMA = HG * T
    SCORES = HG * T
    ADDS = HG * (T - 1)
    STACK_DMAS = 12
    SPLITS = 16
    LN_STEPS = 3 * T + 1
    CONSTS = 7

    plain = batch_work(False, False)
    of_batch = {0: batch_work(True, False), B - 1: batch_work(False, True)}

    def items_of(b):
        return of_batch.get(b, plain) if isinstance(b, int) else plain

    def work_before(b):
        if isinstance(b, int) and b == 0:
            return len(PROLOGUE)
        return b * len(plain) + (len(PROLOGUE) + len(of_batch[0]) - len(plain))

    def splits_before(b):
        return b * SPLITS + sum(k in "hqkm" for k in PROLOGUE)

    def item_number(b, g, s, n):
        items = items_of(b)
        k = [i for i, it in enumerate(items) if it[:2] == (g, s)][n]
        split = sum(it[2] in "hqkm" for it in items[:k])
        return k, split

    def slot_items(b, g, s):
        return [(n, it[2], it[3]) for n, it in
                enumerate(it for it in items_of(b) if it[:2] == (g, s))]

    with ExitStack() as ctx:
        def sb(name, shape, dt):
            return ctx.enter_context(nc.sbuf_tensor(name, shape, dt))

        def bank(name):
            return ctx.enter_context(nc.psum_tensor(name, [P, 512], F32))

        def sem(name):
            return ctx.enter_context(nc.semaphore(name))

        w_hi = {n: sb(f"w{n}_hi", [P, C, D], F32R) for n in "qkvo"}
        w_lo = {n: sb(f"w{n}_lo", [P, C, D], F32R) for n in "qkvo"}
        q_stack = sb("q_stack", [P, STACK_SLOTS, HG, S], F32R)
        k_stack = sb("k_stack", [P, STACK_SLOTS, HG, S], F32R)
        part_hi = sb("part_hi", [P, S], F32R)
        part_lo = sb("part_lo", [P, S], F32R)
        probs = sb("probs", [P, 2, HG, S], F32)
        prob_sum = sb("prob_sum", [P, HG, S], F32)
        h_hi = sb("h_hi", [P, C, S], F32R)
        h_lo = sb("h_lo", [P, C, S], F32R)
        v_sb = sb("v_sb", [P, T, D], F32)
        x_sb = sb("x_sb", [P, T, D], F32)
        adj_sb = sb("adj_sb", [P, T, S], I32)
        mask_q = sb("mask_q", [P, T, S], BF16)
        mask_k = sb("mask_k", [P, T, S], BF16)
        attn_hi = sb("attn_hi", [P, G, S], F32R)
        attn_lo = sb("attn_lo", [P, G, S], F32R)
        attn = sb("attn", [P, S], F32)
        recip = sb("recip", [P, S], F32)
        res = sb("res", [P, T, D], F32)
        bo_all = sb("bo_all", [P, D], F32)
        bias = {n: sb(f"bias_{n}", [P, G], F32) for n in "qkv"}
        identb = sb("identb", [P, P], BF16)
        identf = sb("identf", [P, P], F32)
        ones = sb("ones", [P, DH], F32)
        top = sb("top", [P, MAXIMA], F32)
        top_hi = sb("top_hi", [MAXIMA, P], F32R)
        top_lo = sb("top_lo", [MAXIMA, P], F32R)
        stats = sb("stats", [P, T, 6], F32)
        moments = sb("moments", [P, T, 2], F32)
        var_eps = sb("var_eps", [P, T], F32)
        rstd = sb("rstd", [P, T], F32)
        minus_half = sb("minus_half", [P, T], F32)

        work = [bank("work0"), bank("work1")]
        max_bank = [bank("max0"), bank("max1")]
        score_bank = [bank("score0"), bank("score1")]
        value_bank = bank("value")
        sum_bank = bank("sum")

        x_in, adj_in, bias_in, res_in = map(sem, ["x_in", "adj_in", "bias_in", "res_in"])
        w_in = [sem("w_in0"), sem("w_in1")]
        stack_in, rows_in, out_stored = map(sem, ["stack_in", "rows_in", "out_stored"])
        consts, w_hi_done, w_split = map(sem, ["consts", "w_hi_done", "w_split"])
        ln_step, rstd_ready, mask_ready, res_ready = map(sem, ["ln_step", "rstd_ready", "mask_ready", "res_ready"])
        work_full, hi_ready, split_ready = map(sem, ["work_full", "hi_ready", "split_ready"])
        v_ready, mask_k_ready, out_ready = map(sem, ["v_ready", "mask_k_ready", "out_ready"])
        passed = sem("passed")
        max_full, max_done = map(sem, ["max_full", "max_done"])
        score_full, exp_done, value_done = map(sem, ["score_full", "exp_done", "value_done"])
        add_done, sum_done, recip_done = map(sem, ["add_done", "sum_done", "recip_done"])
        value_copied, attn_scaled, attn_hi_ready, attn_ready = map(
            sem, ["value_copied", "attn_scaled", "attn_hi_ready", "attn_ready"])

        def wait(eng, s, value):
            if not (isinstance(value, int) and value <= 0):
                eng.wait_ge(s, value)

        def wait_alone(eng, s, value):
            eng.wait_ge(s, value)
            eng.sem_inc(passed, 1)

        def batches(eng):
            yield 0, 0
            with eng.Fori(0, TURNS) as i:
                for r in range(3):
                    yield i * 3 + (1 + r), (G * (1 + r)) % STACK_SLOTS
            for b in range(1 + 3 * TURNS, B):
                yield b, (G * b) % STACK_SLOTS

        def work_bank(b, g, s, n):
            return work[(len(PROLOGUE) + item_number(b, g, s, n)[0]) % 2]

        block = ctx.enter_context(nc.Block())

        @block.sync
        def _(sp):
            def load_rows(b):
                for t in range(T):
                    sp.dma_start(x_sb[:, t, :], x[b, t * P:(t + 1) * P, :]).then_inc(x_in, DMA)

            def load_adj(b):
                for t in range(T):
                    sp.dma_start(adj_sb[:, t, :], adj[b, t * P:(t + 1) * P, :]).then_inc(adj_in, DMA)

            def load_residual(b):
                for t in range(T):
                    sp.dma_start(res[:, t, :], x[b, t * P:(t + 1) * P, :]).then_inc(res_in, DMA)

            def store(b, t):
                sp.wait_ge(out_ready, b * T + (t + 1))
                sp.dma_start(out[b, t * P:(t + 1) * P, :], res[:, t, :]).then_inc(out_stored, DMA)

            def stack(kind, slot, count):
                sp.wait_ge(split_ready, count)
                rows = {"q": (part_hi, part_lo, part_hi), "k": (part_hi, part_hi, part_lo)}[kind]
                to = q_stack if kind == "q" else k_stack
                for r, src in enumerate(rows):
                    for j in range(HG):
                        sp.dma_start(to[DH * r:DH * (r + 1), slot, j, :].bitcast(F32),
                                     src[DH * j:DH * (j + 1), :].bitcast(F32)).then_inc(stack_in, DMA)

            def maxima_rows(slot, count):
                sp.wait_ge(split_ready, count)
                for r, src in enumerate((top_hi, top_lo)):
                    row = 3 * DH + r
                    sp.dma_start(q_stack[row:row + 1, slot, :, :].bitcast(F32),
                                 src[:, :].bitcast(F32)).then_inc(rows_in, DMA)

            load_rows(0)
            for n, w in enumerate((Wq, Wk)):
                sp.dma_start(probs[:, n, :, :], w.rearrange("(c p) n -> p c n", p=P)).then_inc(w_in[n], DMA)
            for n, v in (("q", bq), ("k", bk), ("v", bv)):
                sp.dma_start(bias[n][:, :], v.rearrange("(g p) -> p g", p=P),
                             allow_slow_non_contiguous=True).then_inc(bias_in, DMA)
            sp.dma_start(bo_all[:, :], bass.AP(tensor=bo.tensor, offset=bo.offset,
                                               ap=[[0, P], [1, D]])).then_inc(bias_in, DMA)
            load_adj(0)
            for n, w in enumerate((Wv, Wo)):
                sp.wait_ge(w_split, n + 1)
                sp.dma_start(probs[:, n, :, :], w.rearrange("(c p) n -> p c n", p=P)).then_inc(w_in[n], DMA)
            count = 0
            for n, kind in enumerate(PROLOGUE):
                count += kind in "hqkm"
                if kind in "qk":
                    stack(kind, (n - 4) // 2, count)
                if kind == "m":
                    maxima_rows(0, count)

            for b, slot0 in batches(sp):
                last = isinstance(b, int) and b == B - 1
                first = isinstance(b, int) and b == 0
                for g in range(4):
                    for s in range(4):
                        for n, kind, _ in slot_items(b, g, s):
                            count = splits_before(b) + item_number(b, g, s, n)[1] + 1
                            if kind in "qk":
                                stack(kind, (slot0 + g + 2) % STACK_SLOTS, count)
                            if kind == "m":
                                maxima_rows((slot0 + g + 1) % STACK_SLOTS, count)
                        if (g, s) == (0, 0) and not last:
                            sp.wait_ge(work_full, work_before(b) - (0 if not first else 5))
                            load_rows(b + 1)
                        if (g, s) == (0, 1) and not last:
                            sp.wait_ge(mask_ready, b * T + T)
                            load_adj(b + 1)
                        if (g, s) == (0, 2) and not first:
                            wait(sp, out_stored, b * (T * DMA) - T * DMA if not (isinstance(b, int) and b == 1) else 0)
                            load_residual(b - 1)
                        if not first:
                            if g == 1 and s >= 1:
                                store(b - 1, s - 1)
                            if (g, s) == (2, 0):
                                store(b - 1, T - 1)
            sp.wait_ge(out_stored, (B - 1) * T * DMA)
            load_residual(B - 1)
            for t in range(T):
                store(B - 1, t)
            sp.wait_ge(out_stored, B * T * DMA)

        @block.gpsimd
        def _(pool):
            pool.memset(identb[:, :], 0.0).then_inc(consts, 1)
            pool.memset(identf[:, :], 0.0).then_inc(consts, 1)
            pool.wait_ge(consts, 2)
            for ident in (identb, identf):
                pool.affine_select(out=ident[:, :], in_=ident[:, :], compare_op=ALU.not_equal, fill=1.0,
                                   base=0, pattern=[[-1, P]], channel_multiplier=1).then_inc(consts, 1)
            pool.memset(ones[:, :], 1.0).then_inc(consts, 1)
            pool.memset(minus_half[:, :], -0.5).then_inc(consts, 1)
            pool.wait_ge(consts, CONSTS - 1)
            pool.memset(k_stack[3 * DH:P, :, :, :].bitcast(F32), 1.0).then_inc(consts, 1)
            pool.wait_ge(consts, CONSTS)

            def reciprocal_std(b):
                pool.wait_ge(ln_step, b * LN_STEPS + (2 * T + 1))
                pool.tensor_tensor(rstd[:, :], var_eps[:, :], minus_half[:, :], ALU.pow).then_inc(rstd_ready, 1)

            def add_output_bias(b):
                pool.wait_ge(bias_in, 4 * DMA)
                pool.wait_ge(res_in, b * (T * DMA) + T * DMA)
                for t in range(T):
                    pool.tensor_tensor(res[:, t, :], res[:, t, :], bo_all[:, :], ALU.add).then_inc(res_ready, 1)

            def add_tiles(b, g, s):
                u = b * G + g
                for j in range(HG):
                    pool.wait_ge(exp_done, u * SCORES + (s * HG + j + 1))
                    if s == 1:
                        wait(pool, sum_done, u)
                        pool.tensor_tensor(prob_sum[:, j, :], probs[:, 0, j, :], probs[:, 1, j, :],
                                           ALU.add).then_inc(add_done, 1)
                    else:
                        pool.wait_ge(add_done, u * ADDS + ((s - 2) * HG + j + 1))
                        pool.tensor_tensor(prob_sum[:, j, :], prob_sum[:, j, :], probs[:, s % 2, j, :],
                                           ALU.add).then_inc(add_done, 1)

            reciprocal_std(0)
            for b, _ in batches(pool):
                last = isinstance(b, int) and b == B - 1
                first = isinstance(b, int) and b == 0
                for g in range(4):
                    if g == 1 and not first:
                        add_output_bias(b - 1)
                    for s in range(1, 4):
                        add_tiles(b, g, s)
                        if (g, s) == (0, 3) and not last:
                            reciprocal_std(b + 1)
            add_output_bias(B - 1)

        @block.scalar
        def _(act):
            for n, name in enumerate("qkvo"):
                act.wait_ge(w_in[n % 2], DMA * (n // 2 + 1))
                act.copy(w_hi[name][:, :, :], probs[:, n % 2, :, :]).then_inc(w_hi_done, 1)
            act.wait_ge(bias_in, 4 * DMA)

            def evacuate(kind, nth, bank_, number, stacked):
                if kind == "o":
                    return
                act.wait_ge(work_full, number + 1)
                if kind in "qk":
                    wait(act, stack_in, stacked)
                    act.activation(part_hi[:, :], bank_[:, :], ACT.Identity,
                                   bias=bias[kind][:, nth:nth + 1]).then_inc(hi_ready, 1)
                if kind == "h":
                    act.activation(h_hi[:, :, nth * P:(nth + 1) * P],
                                   bank_[:, :].rearrange("p (c n) -> p c n", c=C), ACT.Relu).then_inc(hi_ready, 1)
                if kind == "m":
                    wait(act, rows_in, stacked)
                    act.activation(top_hi[:, :], bank_[0:MAXIMA, 0:P], ACT.Copy, scale=-1.0).then_inc(hi_ready, 1)
                if kind == "v":
                    act.copy(v_sb[:, nth, :], bank_[:, :]).then_inc(v_ready, 1)
                if kind == "b":
                    act.activation(mask_k[:, nth, :], bank_[:, 0:S // 2].bitcast(BF16), ACT.Copy,
                                   scale=MASKED_EXP).then_inc(mask_k_ready, 1)

            seen = {}
            for n, kind in enumerate(PROLOGUE):
                nth = seen.get(kind, 0)
                stacked = (seen.get("q", 0) + seen.get("k", 0)) * STACK_DMAS * DMA if kind in "qk" else 0
                evacuate(kind, nth, work[n % 2], n, stacked)
                seen[kind] = nth + 1

            def exponentials(b, g, s):
                u = b * G + g
                wait(act, value_done, u * T + (s - 1))
                for j in range(HG):
                    wait(act, add_done, u * ADDS + {0: 5 + j - ADDS, 1: 9 + j - ADDS, 2: j + 1, 3: j + 1}[s])
                    act.wait_ge(score_full, u * SCORES + (s * HG + j + 1))
                    act.activation(probs[:, s % 2, j, :], score_bank[j % 2][:, :], ACT.Exp,
                                   scale=SCALE).then_inc(exp_done, 1)

            def copy_values(u):
                act.wait_ge(value_done, u * T + T)
                wait(act, attn_ready, u)
                act.copy(attn[:, :], value_bank[:, :]).then_inc(value_copied, 1)

            def attention_hi(u, g):
                act.wait_ge(attn_scaled, u + 1)
                act.activation(attn_hi[:, g, :], attn[:, :], ACT.Identity,
                               bias=bias["v"][:, g:g + 1]).then_inc(attn_hi_ready, 1)

            for b, _ in batches(act):
                first = isinstance(b, int) and b == 0
                for g in range(4):
                    for s in range(4):
                        u = b * G + g
                        exponentials(b, g, s)
                        for n, kind, nth in slot_items(b, g, s):
                            k, _ = item_number(b, g, s, n)
                            group = (g + 2) % 4 if kind in "qk" else nth
                            stacked = ((u + 2) * 2 + (kind == "k")) * (STACK_DMAS * DMA) if kind in "qk" \
                                else (u + 1) * (2 * DMA)
                            evacuate(kind, group, work_bank(b, g, s, n), work_before(b) + k, stacked)
                        if first and g == 0:
                            continue
                        if s == 0:
                            copy_values(u - 1)
                        if s == 3:
                            if g == 1 and not first:
                                k = max(i for i, it in enumerate(items_of(b)) if it[2] == "o")
                                act.wait_ge(work_full, work_before(b) + (k + 1))
                            attention_hi(u - 1, (g - 1) % 4)
            copy_values(B * G - 1)
            attention_hi(B * G - 1, G - 1)

        @block.vector
        def _(dve):
            def layernorm_stats(b, tiles):
                dve.wait_ge(x_in, b * (T * DMA) + T * DMA)
                for t in tiles:
                    dve.bn_stats(stats[:, t, :], x_sb[:, t, :]).then_inc(ln_step, 1)
                wait_alone(dve, ln_step, b * LN_STEPS + (2 * tiles[0] + 2))
                for t in tiles:
                    dve.bn_aggr(moments[:, t, :], stats[:, t, :]).then_inc(ln_step, 1)

            def layernorm_var(b):
                dve.wait_ge(ln_step, b * LN_STEPS + 2 * T)
                wait(dve, rstd_ready, b)
                dve.tensor_scalar(var_eps[:, :], moments[:, :, 1], EPS, None, ALU.add).then_inc(ln_step, 1)

            def layernorm_apply(b):
                dve.wait_ge(rstd_ready, b + 1)
                for t in range(T):
                    dve.tensor_scalar(x_sb[:, t, :], x_sb[:, t, :], moments[:, t, 0:1], rstd[:, t:t + 1],
                                      ALU.subtract, ALU.mult).then_inc(ln_step, 1)

            def convert_mask(b):
                dve.wait_ge(adj_in, b * (T * DMA) + T * DMA)
                wait(dve, max_done, b * (G * MAXIMA))
                wait(dve, work_full, 0 if isinstance(b, int) and b == 0 else work_before(b - 1))
                for t in range(T):
                    dve.tensor_scalar(mask_q[:, t, :], adj_sb[:, t, :], 0, MASKED, ALU.is_equal,
                                      ALU.mult).then_inc(mask_ready, 1)

            def maxima(u, batch_next, first, count):
                for n in range(first, first + count):
                    if n == 0:
                        dve.wait_ge(mask_ready, batch_next * T + T)
                    wait_alone(dve, max_full, u * MAXIMA + (n + 1))
                    t, j = n // HG, n % HG
                    dve.tensor_tensor_reduce(max_bank[n % 2][:, :], max_bank[n % 2][:, :], mask_q[:, t, :],
                                             1.0, NEG_MAX, ALU.add, ALU.max,
                                             top[:, j * T + t:j * T + t + 1]).then_inc(max_done, 1)

            def evacuate(kind, nth, bank_, number, splits, b_out):
                if kind in "qkhm":
                    dve.wait_ge(hi_ready, splits + 1)
                if kind in "qk":
                    dve.scalar_tensor_tensor(part_lo[:, :], bank_[:, :], bias[kind][:, nth:nth + 1], part_hi[:, :],
                                             ALU.add, ALU.subtract).then_inc(split_ready, 1)
                if kind == "h":
                    rows = slice(nth * P, (nth + 1) * P)
                    dve.scalar_tensor_tensor(h_lo[:, :, rows], bank_[:, :].rearrange("p (c n) -> p c n", c=C), 0.0,
                                             h_hi[:, :, rows], ALU.max, ALU.subtract).then_inc(split_ready, 1)
                if kind == "m":
                    dve.scalar_tensor_tensor(top_lo[:, :], bank_[0:MAXIMA, 0:P], -1.0, top_hi[:, :],
                                             ALU.mult, ALU.subtract).then_inc(split_ready, 1)
                if kind == "o":
                    dve.wait_ge(work_full, number + 1)
                    dve.wait_ge(res_ready, b_out * T + (nth + 1))
                    dve.tensor_tensor(res[:, nth, :], bank_[:, :], res[:, nth, :], ALU.add).then_inc(out_ready, 1)

            def normalise(u):
                dve.wait_ge(sum_done, u + 1)
                wait(dve, attn_scaled, u)
                dve.reciprocal(recip[:, :], sum_bank[:, :]).then_inc(recip_done, 1)
                dve.wait_ge(recip_done, u + 1)
                dve.wait_ge(value_copied, u + 1)
                dve.tensor_tensor(attn[:, :], attn[:, :], recip[:, :], ALU.mult).then_inc(attn_scaled, 1)

            def attention_lo(u, g):
                dve.wait_ge(attn_hi_ready, u + 1)
                dve.scalar_tensor_tensor(attn_lo[:, g, :], attn[:, :], bias["v"][:, g:g + 1], attn_hi[:, g, :],
                                         ALU.add, ALU.subtract).then_inc(attn_ready, 1)

            def split_weights(names):
                for name in names:
                    n = "qkvo".index(name)
                    dve.wait_ge(w_hi_done, n + 1)
                    dve.tensor_tensor(w_lo[name][:, :, :], probs[:, n % 2, :, :], w_hi[name][:, :, :],
                                      ALU.subtract).then_inc(w_split, 1)

            layernorm_stats(0, (0, 1))
            layernorm_stats(0, (2, 3))
            layernorm_var(0)
            layernorm_apply(0)
            split_weights("q")
            split_weights("k")
            convert_mask(0)
            dve.wait_ge(bias_in, 4 * DMA)
            seen, splits = {}, 0
            for n, kind in enumerate(PROLOGUE):
                if kind == "m":
                    split_weights("vo")
                    maxima(0, 0, 0, MAXIMA)
                nth = seen.get(kind, 0)
                evacuate(kind, nth, work[n % 2], n, splits, None)
                seen[kind] = nth + 1
                splits += kind in "hqkm"

            for b, _ in batches(dve):
                first = isinstance(b, int) and b == 0
                last = isinstance(b, int) and b == B - 1
                for g in range(4):
                    for s in range(4):
                        u = b * G + g
                        if s == 0 and not (first and g < 2):
                            attention_lo(u - 2, (g - 2) % 4)
                        share = 0 if last and g == 3 else MAX_SHARE[s]
                        begun = min(4, share)
                        at = MAX_FIRST[s]
                        batch_next = b + 1 if g == 3 else b
                        maxima(u + 1, batch_next, at, begun)
                        for n, kind, nth in slot_items(b, g, s):
                            if begun < share:
                                maxima(u + 1, batch_next, at + begun, 1)
                                begun += 1
                            k, splits = item_number(b, g, s, n)
                            group = (g + 2) % 4 if kind in "qk" else nth
                            evacuate(kind, group, work_bank(b, g, s, n), work_before(b) + k,
                                     splits_before(b) + splits, b - 1)
                        if begun < share:
                            maxima(u + 1, batch_next, at + begun, share - begun)
                        if not last:
                            if (g, s) == (0, 1):
                                layernorm_stats(b + 1, (0, 1))
                            if (g, s) == (0, 2):
                                layernorm_stats(b + 1, (2, 3))
                                layernorm_var(b + 1)
                            if (g, s) == (1, 0):
                                layernorm_apply(b + 1)
                            if (g, s) == (2, 3):
                                convert_mask(b + 1)
                        if s == 3 and not (first and g == 0):
                            normalise(u - 1)
            attention_lo(B * G - 2, G - 2)
            normalise(B * G - 1)
            attention_lo(B * G - 1, G - 1)
            for t in range(T):
                number = work_before(B - 1) + len(of_batch[B - 1]) + t
                evacuate("o", t, work[(len(PROLOGUE) + len(of_batch[B - 1]) + t) % 2], number, None, B - 1)

        @block.tensor
        def _(pe):
            def project(to, pairs, done):
                for n, (lhs, rhs) in enumerate(pairs):
                    mm = pe.matmul(to[:, :], lhs, rhs, start=(n == 0), stop=(n == len(pairs) - 1))
                mm.then_inc(done, 1)

            def do_work(kind, nth, bank_, b, u):
                cols = slice(nth * P, (nth + 1) * P)
                if kind in "qk":
                    hi, lo = w_hi[kind], w_lo[kind]
                    project(bank_, [pair for c in range(C) for pair in
                                    ((hi[:, c, cols], h_hi[:, c, :]), (hi[:, c, cols], h_lo[:, c, :]),
                                     (lo[:, c, cols], h_hi[:, c, :]))], work_full)
                if kind == "v":
                    project(bank_, [pair for c in range(C) for pair in
                                    ((h_hi[:, c, cols], w_hi["v"][:, c, :]), (h_hi[:, c, cols], w_lo["v"][:, c, :]),
                                     (h_lo[:, c, cols], w_hi["v"][:, c, :]))], work_full)
                if kind == "o":
                    project(bank_, [pair for c in range(C) for pair in
                                    ((attn_hi[:, c, cols], w_hi["o"][:, c, :]), (attn_hi[:, c, cols], w_lo["o"][:, c, :]),
                                     (attn_lo[:, c, cols], w_hi["o"][:, c, :]))], work_full)
                if kind == "h":
                    for c in range(C):
                        mm = pe.transpose(bank_[:, c * P:(c + 1) * P], x_sb[:, nth, c * P:(c + 1) * P], identf[:, :])
                    mm.then_inc(work_full, 1)
                if kind == "b":
                    tile = bank_[:, 0:S // 2].bitcast(BF16)
                    for t in range(T):
                        mm = pe.transpose(tile[:, t * P:(t + 1) * P], mask_q[:, t, cols], identb[:, :])
                    mm.then_inc(work_full, 1)
                if kind == "m":
                    pe.transpose(bank_[0:MAXIMA, 0:P], top[:, :], identf[:, :]).then_inc(work_full, 1)

            def maxima(u, slot, first, count):
                for n in range(first, first + count):
                    if n == 0:
                        pe.wait_ge(stack_in, (u + 1) * (2 * STACK_DMAS * DMA))
                    wait(pe, max_done, u * MAXIMA + (n - 1))
                    t, j = n // HG, n % HG
                    pe.matmul(max_bank[n % 2][:, :], q_stack[0:3 * DH, slot, j, t * P:(t + 1) * P],
                              k_stack[0:3 * DH, slot, j, :], start=True, stop=True).then_inc(max_full, 1)

            def score(b, g, s, j, slot):
                u = b * G + g
                if j == 0 and s == 0:
                    pe.wait_ge(rows_in, (u + 1) * (2 * DMA))
                if j == 0 and g == 0:
                    pe.wait_ge(mask_k_ready, b * T + (s + 1))
                wait(pe, exp_done, u * SCORES + (s * HG + j - 1))
                to = score_bank[j % 2]
                pe.matmul(to[:, :], identb[:, :], mask_k[:, s, :], start=True, stop=False)
                pe.matmul(to[:, :], k_stack[0:3 * DH + 2, slot, j, s * P:(s + 1) * P],
                          q_stack[0:3 * DH + 2, slot, j, :], start=False, stop=True).then_inc(score_full, 1)

            def values(b, g, s):
                u = b * G + g
                pe.wait_ge(exp_done, u * SCORES + (s * HG + HG))
                if g == 0:
                    pe.wait_ge(v_ready, b * T + (s + 1))
                if s == 0:
                    wait(pe, value_copied, u)
                for j in range(HG):
                    h = g * HG + j
                    mm = pe.matmul(value_bank[DH * j:DH * (j + 1), :], v_sb[:, s, h * DH:(h + 1) * DH],
                                   probs[:, s % 2, j, :], start=(s == 0), stop=(s == T - 1))
                mm.then_inc(value_done, 1)

            def sums(u):
                pe.wait_ge(add_done, u * ADDS + ADDS)
                wait(pe, recip_done, u)
                for j in range(HG):
                    mm = pe.matmul(sum_bank[DH * j:DH * (j + 1), :], ones[:, :], prob_sum[:, j, :],
                                   start=True, stop=True)
                mm.then_inc(sum_done, 1)

            emptied = {"v": v_ready, "b": mask_k_ready, "o": out_ready}

            def wait_bank(b, k):
                items = items_of(b)
                if k < 2:
                    if k == 0:
                        pe.wait_ge(split_ready, splits_before(b))
                    else:
                        pe.wait_ge(mask_k_ready, b * T + T)
                    return
                _, _, kind, nth = items[k - 2]
                if kind in emptied:
                    before = {"v": b * T, "b": b * T + T, "o": (b - 1) * T}[kind]
                    pe.wait_ge(emptied[kind], before + (nth + 1))
                else:
                    done = sum(it[2] in "hqkm" for it in items[:k - 2]) + 1
                    pe.wait_ge(split_ready, splits_before(b) + done)

            def run_item(b, g, s, n, kind, nth):
                k, _ = item_number(b, g, s, n)
                wait_bank(b, k)
                u = b * G + g
                if kind == "h":
                    pe.wait_ge(ln_step, b * LN_STEPS + 2 * LN_STEPS)
                if kind == "q" and g == 2:
                    done = max(i for i, it in enumerate(items_of(b)) if it[2] == "h") + 1
                    pe.wait_ge(split_ready, splits_before(b) + sum(it[2] in "hqkm" for it in items_of(b)[:done]))
                if kind == "b":
                    pe.wait_ge(mask_ready, b * T + 2 * T)
                if kind == "m":
                    pe.wait_ge(max_done, u * MAXIMA + 2 * MAXIMA)
                if kind == "o":
                    pe.wait_ge(attn_ready, b * G)
                group = (g + 2) % 4 if kind in "qk" else nth
                do_work(kind, 0 if kind == "m" else group, work_bank(b, g, s, n), b, u)

            pe.wait_ge(consts, CONSTS)
            seen = {}
            for n, kind in enumerate(PROLOGUE):
                nth = seen.get(kind, 0)
                if n >= 2:
                    prev = PROLOGUE[n - 2]
                    count = sum(k in "hqkm" if prev in "hqkm" else k == prev for k in PROLOGUE[:n - 1])
                    pe.wait_ge(mask_k_ready if prev == "b" else split_ready, count)
                if kind == "h":
                    pe.wait_ge(ln_step, LN_STEPS)
                if kind in "qk":
                    pe.wait_ge(split_ready, T)
                    pe.wait_ge(w_split, 1 if kind == "q" else 2)
                if kind == "b":
                    pe.wait_ge(mask_ready, T)
                if kind == "m":
                    maxima(0, 0, 0, MAXIMA)
                    pe.wait_ge(max_done, MAXIMA)
                do_work(kind, 0 if kind == "m" else nth, work[n % 2], 0, 0)
                seen[kind] = nth + 1
            pe.wait_ge(w_split, 4)

            for b, slot0 in batches(pe):
                first = isinstance(b, int) and b == 0
                last = isinstance(b, int) and b == B - 1
                for g in range(4):
                    u = b * G + g
                    slot, slot_next = (slot0 + g) % STACK_SLOTS, (slot0 + g + 1) % STACK_SLOTS
                    for s in range(4):
                        share = 0 if last and g == 3 else MAX_SHARE[s]
                        at = MAX_FIRST[s]
                        begun = 0
                        for j in range(HG):
                            score(b, g, s, j, slot)
                            if begun < share:
                                maxima(u + 1, slot_next, at + begun, 1)
                                begun += 1
                        for n, kind, nth in slot_items(b, g, s):
                            run_item(b, g, s, n, kind, nth)
                            if begun < share:
                                maxima(u + 1, slot_next, at + begun, 1)
                                begun += 1
                        if begun < share:
                            maxima(u + 1, slot_next, at + begun, share - begun)
                        if s > 0:
                            values(b, g, s - 1)
                        elif not (first and g == 0):
                            values(b if g > 0 else b - 1, (g - 1) % 4, T - 1)
                            sums(u - 1)
            values(B - 1, G - 1, T - 1)
            sums(B * G - 1)
            pe.wait_ge(attn_ready, B * G)
            for t in range(T):
                k = len(of_batch[B - 1]) + t
                if t >= 2:
                    pe.wait_ge(out_ready, (B - 1) * T + (t - 1))
                elif t == 0:
                    pe.wait_ge(split_ready, splits_before(B - 1) + sum(it[2] in "hqkm" for it in of_batch[B - 1]))
                    pe.wait_ge(out_ready, (B - 1) * T)
                do_work("o", t, work[(len(PROLOGUE) + k) % 2], B - 1, None)


_INS = ["x", "adj", "L0_gnn_Wq", "L0_gnn_bq", "L0_gnn_Wk", "L0_gnn_bk", "L0_gnn_Wv", "L0_gnn_bv",
        "L0_gnn_Wo", "L0_gnn_bo"]


def kernel(**inputs):
    import numpy as _np
    import concourse.bacc as _bacc
    from concourse import mybir as _mybir
    from concourse.bass_utils import run_bass_kernel_spmd as _run

    nc = _bacc.Bacc("TRN2", target_bir_lowering=False, num_devices=1, dynamic_dma_scratch_size=1024)
    arrays, args = {}, []
    for name in _INS:
        a = _np.ascontiguousarray(inputs[name])
        arrays[f"in_{name}_dram"] = a
        args.append(nc.dram_tensor(f"in_{name}_dram", a.shape, _mybir.dt.from_np(a.dtype), kind="ExternalInput").ap())
    shape = inputs["x"].shape
    args.append(nc.dram_tensor("out_0_dram", shape, _mybir.dt.float32, kind="ExternalOutput").ap())
    build_kernel(nc, *args)
    r = _run(nc, [arrays], core_ids=[0])
    return r.results[0]["out_0_dram"]
```

```python
from contextlib import ExitStack

import concourse.bass as bass
from concourse import mybir

ALU = mybir.AluOpType
ACT = mybir.ActivationFunctionType
F32 = mybir.dt.float32
F32R = mybir.dt.float32r
BF16 = mybir.dt.bfloat16
I32 = mybir.dt.int32

P = 128
HEADS = 16
DH = 32
HG = P // DH
STACK_SLOTS = 3
MASKED = -(2.0 ** 100)
MASKED_EXP = 2.0
NEG_MAX = -3.0e38
EPS = 1e-5
DMA = 16

WORK = {(g, s): [] for g in range(4) for s in range(4)}
for _g in range(4):
    WORK[_g, 0] += ["q"]
    WORK[_g, 1] += ["k"]
    WORK[_g, 3] += ["m"]
WORK[0, 2] += ["v"]
WORK[0, 3] += ["v"]
WORK[1, 1] += ["h"]
WORK[1, 2] += ["h", "o", "h"]
WORK[1, 3] += ["o", "h"]
WORK[2, 2] += ["o"]
WORK[2, 3] += ["o"]
WORK[3, 1] += ["b"]
WORK[3, 2] += ["w", "b"]
WORK[3, 3] += ["w", "b", "b"]
for _g in range(4):
    WORK[_g, 0] += ["d"]
PROLOGUE = list("hhhhqkqkwwbbmbb")
ATTENTION_SLOT = [2, 1, 3, 2]
MAX_SHARE = [6, 6, 4, 0]
MAX_FIRST = [0, 6, 12, 16]
MAX_BANKS = 3
M_AFTER = 0


def batch_work(first, last):
    items, seen = [], {}
    for g in range(4):
        for s in range(4):
            for kind in WORK[g, s]:
                if first and (kind == "o" or (kind == "d" and g == 0)):
                    continue
                if last and (kind in "hbw" or (kind in "qk" and g >= 2) or (kind == "m" and g == 3)):
                    continue
                items.append((g, s, kind, seen.get(kind, 0)))
                seen[kind] = seen.get(kind, 0) + 1
    return items


def build_kernel(nc, x, adj, Wq, bq, Wk, bk, Wv, bv, Wo, bo, out):
    B, S, D = x.shape
    T = S // P
    C = D // P
    G = HEADS // HG
    assert T == 4 and C == 4 and G == 4 and D == HEADS * DH and (B - 4) % 3 == 0
    TURNS = (B - 4) // 3
    SCALE = float(DH) ** -0.5
    MAXIMA = HG * T
    SCORES = HG * T
    ADDS = HG * (T - 1)
    STACK_DMAS = 12
    SPLITS = 16
    LN_STEPS = 3 * T + 1
    CONSTS = 7

    plain = batch_work(False, False)
    of_batch = {0: batch_work(True, False), B - 1: batch_work(False, True)}
    assert len(plain) % 2 == 0

    def items_of(b):
        return of_batch.get(b, plain) if isinstance(b, int) else plain

    def work_before(b):
        if isinstance(b, int) and b == 0:
            return len(PROLOGUE)
        return b * len(plain) + (len(PROLOGUE) + len(of_batch[0]) - len(plain))

    def splits_before(b):
        return b * SPLITS + sum(k in "hqkm" for k in PROLOGUE)

    def item_number(b, g, s, n):
        items = items_of(b)
        k = [i for i, it in enumerate(items) if it[:2] == (g, s)][n]
        split = sum(it[2] in "hqkm" for it in items[:k])
        return k, split

    def slot_items(b, g, s):
        return [(n, it[2], it[3]) for n, it in
                enumerate(it for it in items_of(b) if it[:2] == (g, s))]

    with ExitStack() as ctx:
        def sb(name, shape, dt):
            return ctx.enter_context(nc.sbuf_tensor(name, shape, dt))

        def bank(name):
            return ctx.enter_context(nc.psum_tensor(name, [P, 512], F32))

        def sem(name):
            return ctx.enter_context(nc.semaphore(name))

        w_hi = {n: sb(f"w{n}_hi", [P, C, D], F32R) for n in "qkvo"}
        w_lo = {n: sb(f"w{n}_lo", [P, C, D], F32R) for n in "qkvo"}
        stacks = sb("stacks", [P, STACK_SLOTS, 2, HG, S], F32R)
        k_stack, q_stack = stacks[:, :, 0, :, :], stacks[:, :, 1, :, :]
        parts = sb("parts", [P, 4, S], F32R)
        part_hi = {"k": parts[:, 0, :], "q": parts[:, 2, :]}
        part_lo = {"k": parts[:, 1, :], "q": parts[:, 3, :]}
        probs = sb("probs", [P, 2, HG, S], F32)
        prob_sum = sb("prob_sum", [P, HG, S], F32)
        h_hi = sb("h_hi", [P, C, S], F32R)
        h_lo = sb("h_lo", [P, C, S], F32R)
        v_sb = sb("v_sb", [P, T, D], F32)
        x_sb = sb("x_sb", [P, T, D], F32)
        mask_q = sb("mask_q", [P, T, S], BF16)
        mask_k = sb("mask_k", [P, T, S], BF16)
        attn_hi = sb("attn_hi", [P, G, S], F32R)
        attn_lo = sb("attn_lo", [P, G, S], F32R)
        attn = sb("attn", [P, 2, S], F32)
        recip = sb("recip", [P, S], F32)
        res = sb("res", [P, T, D], F32)
        bo_all = sb("bo_all", [P, D], F32)
        bias = {n: sb(f"bias_{n}", [P, G], F32) for n in "qkv"}
        identb = sb("identb", [P, P], BF16)
        identf = sb("identf", [P, P], F32)
        ones = sb("ones", [P, DH], F32)
        top = sb("top", [P, MAXIMA], F32)
        top_hi = sb("top_hi", [MAXIMA, P], F32R)
        top_lo = sb("top_lo", [MAXIMA, P], F32R)
        stats = sb("stats", [P, T, 6], F32)
        moments = sb("moments", [P, T, 2], F32)
        var_eps = sb("var_eps", [P, T], F32)
        rstd = sb("rstd", [P, T], F32)
        minus_half = sb("minus_half", [P, T], F32)

        work = [bank("work0"), bank("work1")]
        max_bank = [bank(f"max{n}") for n in range(MAX_BANKS)]
        score_bank = [bank("score0"), bank("score1")]
        value_bank = bank("value")

        x_in, adj_in, bias_in, res_in = map(sem, ["x_in", "adj_in", "bias_in", "res_in"])
        w_in = [sem("w_in0"), sem("w_in1")]
        stack_in, rows_in, out_stored = map(sem, ["stack_in", "rows_in", "out_stored"])
        consts, w_hi_done, w_split = map(sem, ["consts", "w_hi_done", "w_split"])
        ln_step, rstd_ready, mask_ready, res_ready = map(sem, ["ln_step", "rstd_ready", "mask_ready", "res_ready"])
        work_full, hi_ready, split_ready = map(sem, ["work_full", "hi_ready", "split_ready"])
        v_ready, mask_k_ready, out_ready = map(sem, ["v_ready", "mask_k_ready", "out_ready"])
        passed = sem("passed")
        max_full, max_done = map(sem, ["max_full", "max_done"])
        score_full, exp_done, value_done = map(sem, ["score_full", "exp_done", "value_done"])
        add_done, sum_copied, recip_done = map(sem, ["add_done", "sum_copied", "recip_done"])
        value_copied, attn_scaled, attn_hi_ready, attn_ready = map(
            sem, ["value_copied", "attn_scaled", "attn_hi_ready", "attn_ready"])

        def wait(eng, s, value):
            if not (isinstance(value, int) and value <= 0):
                eng.wait_ge(s, value)

        def wait_alone(eng, s, value):
            eng.wait_ge(s, value)
            eng.sem_inc(passed, 1)

        def batches(eng):
            yield 0, 0
            with eng.Fori(0, TURNS) as i:
                for r in range(3):
                    yield i * 3 + (1 + r), (1 + r) % 3
            for b in range(1 + 3 * TURNS, B):
                yield b, b % 3

        def stack_slot(phase, g):
            return (phase + g) % STACK_SLOTS

        def max_bank_of(phase, g, n):
            return max_bank[(phase + g + n) % MAX_BANKS]

        def work_bank(b, g, s, n):
            return bank_number(b, item_number(b, g, s, n)[0])

        def bank_number(b, k):
            before = len(PROLOGUE) + (0 if isinstance(b, int) and b == 0 else len(of_batch[0]))
            return work[(before + k) % 2]

        def adj_sb(b):
            return (res if isinstance(b, int) and b == 0 else x_sb)[:, :, :].bitcast(I32)

        block = ctx.enter_context(nc.Block())

        @block.sync
        def _(sp):
            def load_rows(b):
                for t in range(T):
                    sp.dma_start(x_sb[:, t, :], x[b, t * P:(t + 1) * P, :]).then_inc(x_in, DMA)

            def load_adj(b):
                for t in range(T):
                    sp.dma_start(adj_sb(b)[:, t, :], adj[b, t * P:(t + 1) * P, :]).then_inc(adj_in, DMA)

            def load_residual(b):
                for t in range(T):
                    sp.dma_start(res[:, t, :], x[b, t * P:(t + 1) * P, :]).then_inc(res_in, DMA)

            def store(b, t):
                sp.wait_ge(out_ready, b * T + (t + 1))
                sp.dma_start(out[b, t * P:(t + 1) * P, :], res[:, t, :]).then_inc(out_stored, DMA)

            def stack(slot, count):
                sp.wait_ge(split_ready, count)
                for r, pair in enumerate((slice(0, 3, 2), slice(0, 4, 3), slice(1, 3))):
                    for j in range(HG):
                        sp.dma_start(stacks[DH * r:DH * (r + 1), slot, :, j, :].bitcast(F32),
                                     parts[DH * j:DH * (j + 1), pair, :].bitcast(F32)).then_inc(stack_in, DMA)

            def maxima_rows(slot, count):
                sp.wait_ge(split_ready, count)
                for r, src in enumerate((top_hi, top_lo)):
                    row = 3 * DH + r
                    sp.dma_start(q_stack[row:row + 1, slot, :, :].bitcast(F32),
                                 src[:, :].bitcast(F32)).then_inc(rows_in, DMA)

            load_rows(0)
            for n, w in enumerate((Wq, Wk)):
                sp.dma_start(probs[:, n, :, :], w.rearrange("(c p) n -> p c n", p=P)).then_inc(w_in[n], DMA)
            for n, v in (("q", bq), ("k", bk), ("v", bv)):
                sp.dma_start(bias[n][:, :], v.rearrange("(g p) -> p g", p=P),
                             allow_slow_non_contiguous=True).then_inc(bias_in, DMA)
            sp.dma_start(bo_all[:, :], bass.AP(tensor=bo.tensor, offset=bo.offset,
                                               ap=[[0, P], [1, D]])).then_inc(bias_in, DMA)
            load_adj(0)
            for n, w in enumerate((Wv, Wo)):
                sp.wait_ge(w_split, n + 1)
                sp.dma_start(probs[:, n, :, :], w.rearrange("(c p) n -> p c n", p=P)).then_inc(w_in[n], DMA)
            count = 0
            for n, kind in enumerate(PROLOGUE):
                count += kind in "hqkm"
                if kind == "k":
                    stack((n - 4) // 2, count)
                if kind == "m":
                    maxima_rows(0, count)

            for b, phase in batches(sp):
                last = isinstance(b, int) and b == B - 1
                first = isinstance(b, int) and b == 0
                for g in range(4):
                    for s in range(4):
                        for n, kind, _ in slot_items(b, g, s):
                            count = splits_before(b) + item_number(b, g, s, n)[1] + 1
                            if kind == "k":
                                stack(stack_slot(phase, g + 2), count)
                            if kind == "m":
                                maxima_rows(stack_slot(phase, g + 1), count)
                        if (g, s) == (0, 0) and not last:
                            if first:
                                sp.wait_ge(work_full, T)
                            else:
                                sp.wait_ge(mask_ready, b * T + T)
                            load_rows(b + 1)
                        if (g, s) == (0, 3) and first:
                            sp.wait_ge(mask_ready, T)
                            sp.sem_inc(out_stored, T * DMA)
                        if (g, s) == (0, 3) and not first:
                            sp.wait_ge(out_stored, b * (T * DMA))
                            load_residual(b - 1)
                        if not first:
                            for n, kind, nth in slot_items(b, g, s):
                                if kind == "o":
                                    store(b - 1, nth)
                        if (g, s) == (1, 3) and not last:
                            k = max(i for i, it in enumerate(items_of(b)) if it[2] == "h")
                            sp.wait_ge(work_full, work_before(b) + (k + 1))
                            load_adj(b + 1)
            sp.wait_ge(out_stored, B * T * DMA)
            load_residual(B - 1)
            for t in range(T):
                store(B - 1, t)
            sp.wait_ge(out_stored, (B + 1) * T * DMA)

        @block.gpsimd
        def _(pool):
            pool.memset(identb[:, :], 0.0).then_inc(consts, 1)
            pool.memset(identf[:, :], 0.0).then_inc(consts, 1)
            pool.wait_ge(consts, 2)
            for ident in (identb, identf):
                pool.affine_select(out=ident[:, :], in_=ident[:, :], compare_op=ALU.not_equal, fill=1.0,
                                   base=0, pattern=[[-1, P]], channel_multiplier=1).then_inc(consts, 1)
            pool.memset(ones[:, :], 1.0).then_inc(consts, 1)
            pool.memset(minus_half[:, :], -0.5).then_inc(consts, 1)
            pool.wait_ge(consts, CONSTS - 1)
            pool.memset(stacks[3 * DH:P, :, 0, :, :].bitcast(F32), 1.0).then_inc(consts, 1)
            pool.wait_ge(consts, CONSTS)

            def reciprocal_std(b):
                pool.wait_ge(ln_step, b * LN_STEPS + (2 * T + 1))
                pool.tensor_tensor(rstd[:, :], var_eps[:, :], minus_half[:, :], ALU.pow).then_inc(rstd_ready, 1)

            def add_output_bias(b):
                pool.wait_ge(bias_in, 4 * DMA)
                pool.wait_ge(res_in, b * (T * DMA) + T * DMA)
                for t in range(T):
                    pool.tensor_tensor(res[:, t, :], res[:, t, :], bo_all[:, :], ALU.add).then_inc(res_ready, 1)

            def add_tiles(b, g, s):
                u = b * G + g
                for j in range(HG):
                    pool.wait_ge(exp_done, u * SCORES + (s * HG + j + 1))
                    if s == 1:
                        wait(pool, sum_copied, u)
                        pool.tensor_tensor(prob_sum[:, j, :], probs[:, 0, j, :], probs[:, 1, j, :],
                                           ALU.add).then_inc(add_done, 1)
                    else:
                        pool.wait_ge(add_done, u * ADDS + ((s - 2) * HG + j + 1))
                        pool.tensor_tensor(prob_sum[:, j, :], prob_sum[:, j, :], probs[:, s % 2, j, :],
                                           ALU.add).then_inc(add_done, 1)

            reciprocal_std(0)
            for b, _ in batches(pool):
                last = isinstance(b, int) and b == B - 1
                first = isinstance(b, int) and b == 0
                for g in range(4):
                    if g == 1 and not first:
                        add_output_bias(b - 1)
                    for s in range(1, 4):
                        add_tiles(b, g, s)
                        if (g, s) == (0, 3) and not last:
                            reciprocal_std(b + 1)
            add_output_bias(B - 1)

        @block.scalar
        def _(act):
            for n, name in enumerate("qkvo"):
                act.wait_ge(w_in[n % 2], DMA * (n // 2 + 1))
                act.copy(w_hi[name][:, :, :], probs[:, n % 2, :, :]).then_inc(w_hi_done, 1)
            act.wait_ge(bias_in, 4 * DMA)

            def evacuate(kind, nth, bank_, number, stacked):
                if kind == "o":
                    return
                act.wait_ge(work_full, number + 1)
                if kind in "qk":
                    wait(act, stack_in, stacked)
                    act.activation(part_hi[kind], bank_[:, :], ACT.Identity,
                                   bias=bias[kind][:, nth:nth + 1]).then_inc(hi_ready, 1)
                if kind == "h":
                    act.activation(h_hi[:, :, nth * P:(nth + 1) * P],
                                   bank_[:, :].rearrange("p (c n) -> p c n", c=C), ACT.Relu).then_inc(hi_ready, 1)
                if kind == "m":
                    wait(act, rows_in, stacked)
                    act.activation(top_hi[:, :], bank_[0:MAXIMA, 0:P], ACT.Copy, scale=-1.0).then_inc(hi_ready, 1)
                if kind in "vw":
                    tile = nth + (2 if kind == "v" else 0)
                    act.copy(v_sb[:, tile, :], bank_[:, :]).then_inc(v_ready, 1)
                if kind == "d":
                    wait(act, attn_scaled, stacked)
                    act.copy(recip[:, :], bank_[:, :]).then_inc(sum_copied, 1)
                if kind == "b":
                    act.activation(mask_k[:, nth, :], bank_[:, 0:S // 2].bitcast(BF16), ACT.Copy,
                                   scale=MASKED_EXP).then_inc(mask_k_ready, 1)

            seen = {}
            for n, kind in enumerate(PROLOGUE):
                nth = seen.get(kind, 0)
                stacked = nth * STACK_DMAS * DMA if kind in "qk" else 0
                evacuate(kind, nth, work[n % 2], n, stacked)
                seen[kind] = nth + 1

            def exponential(b, g, s, j):
                u = b * G + g
                if j == 0:
                    wait(act, value_done, u * T + (s - 1))
                wait(act, add_done, u * ADDS + {0: 5 + j - ADDS, 1: 9 + j - ADDS, 2: j + 1, 3: j + 1}[s])
                act.wait_ge(score_full, u * SCORES + (s * HG + j + 1))
                act.activation(probs[:, s % 2, j, :], score_bank[j % 2][:, :], ACT.Exp,
                               scale=SCALE).then_inc(exp_done, 1)

            def copy_values(u, g):
                act.wait_ge(value_done, u * T + T)
                wait(act, attn_ready, u - 1)
                act.copy(attn[:, g % 2, :], value_bank[:, :]).then_inc(value_copied, 1)

            def attention_hi(u, g):
                act.wait_ge(attn_scaled, u + 1)
                act.activation(attn_hi[:, g, :], attn[:, g % 2, :], ACT.Identity,
                               bias=bias["v"][:, g:g + 1]).then_inc(attn_hi_ready, 1)

            def item(b, g, s, n, kind, nth):
                u = b * G + g
                k, _ = item_number(b, g, s, n)
                group = (g + 2) % 4 if kind in "qk" else nth
                free = {"q": (u + 2) * (STACK_DMAS * DMA), "k": (u + 2) * (STACK_DMAS * DMA),
                        "m": (u + 1) * (2 * DMA), "d": u - 1}.get(kind)
                evacuate(kind, group, work_bank(b, g, s, n), work_before(b) + k, free)

            for b, _ in batches(act):
                first = isinstance(b, int) and b == 0
                for g in range(4):
                    for s in range(4):
                        u = b * G + g
                        items = slot_items(b, g, s)
                        for j in range(HG):
                            exponential(b, g, s, j)
                            if j == M_AFTER:
                                for n, kind, nth in items:
                                    if kind == "m":
                                        item(b, g, s, n, kind, nth)
                        if s == ATTENTION_SLOT[g] and g != 2 and not (first and g < 2):
                            attention_hi(u - 2, (g - 2) % 4)
                        for n, kind, nth in items:
                            if kind not in "md":
                                item(b, g, s, n, kind, nth)
                        if s == ATTENTION_SLOT[g] and g == 2:
                            if not first:
                                k = max(i for i, it in enumerate(items_of(b)) if it[2] == "o")
                                act.wait_ge(work_full, work_before(b) + (k + 1))
                            attention_hi(u - 2, (g - 2) % 4)
                        if s == 0 and not (first and g == 0):
                            copy_values(u - 1, (g - 1) % 4)
                            item(b, g, s, *items[-1])
            attention_hi(B * G - 2, G - 2)
            copy_values(B * G - 1, G - 1)
            k = len(of_batch[B - 1])
            evacuate("d", 0, bank_number(B - 1, k), work_before(B - 1) + k, B * G - 1)
            attention_hi(B * G - 1, G - 1)

        @block.vector
        def _(dve):
            def layernorm_stats(b, tiles):
                dve.wait_ge(x_in, b * (T * DMA) + T * DMA)
                for t in tiles:
                    dve.bn_stats(stats[:, t, :], x_sb[:, t, :]).then_inc(ln_step, 1)
                wait_alone(dve, ln_step, b * LN_STEPS + (2 * tiles[0] + 2))
                for t in tiles:
                    dve.bn_aggr(moments[:, t, :], stats[:, t, :]).then_inc(ln_step, 1)

            def layernorm_var(b):
                dve.wait_ge(ln_step, b * LN_STEPS + 2 * T)
                wait(dve, rstd_ready, b)
                dve.tensor_scalar(var_eps[:, :], moments[:, :, 1], EPS, None, ALU.add).then_inc(ln_step, 1)

            def layernorm_apply(b):
                dve.wait_ge(rstd_ready, b + 1)
                for t in range(T):
                    dve.tensor_scalar(x_sb[:, t, :], x_sb[:, t, :], moments[:, t, 0:1], rstd[:, t:t + 1],
                                      ALU.subtract, ALU.mult).then_inc(ln_step, 1)

            def convert_mask(b):
                dve.wait_ge(adj_in, b * (T * DMA) + T * DMA)
                wait(dve, max_done, b * (G * MAXIMA))
                wait(dve, work_full, 0 if isinstance(b, int) and b == 0 else work_before(b - 1))
                for t in range(T):
                    dve.tensor_scalar(mask_q[:, t, :], adj_sb(b)[:, t, :], 0, MASKED, ALU.is_equal,
                                      ALU.mult).then_inc(mask_ready, 1)

            def maxima(u, batch_next, phase, g, first, count):
                for n in range(first, first + count):
                    if n == 0:
                        dve.wait_ge(mask_ready, batch_next * T + T)
                    wait_alone(dve, max_full, u * MAXIMA + (n + 1))
                    t, j = n // HG, n % HG
                    scores = max_bank_of(phase, g, n)
                    dve.tensor_tensor_reduce(scores[:, :], scores[:, :], mask_q[:, t, :],
                                             1.0, NEG_MAX, ALU.add, ALU.max,
                                             top[:, j * T + t:j * T + t + 1]).then_inc(max_done, 1)

            def evacuate(kind, nth, bank_, number, splits, b_out):
                if kind in "qkhm":
                    dve.wait_ge(hi_ready, splits + 1)
                if kind in "qk":
                    dve.scalar_tensor_tensor(part_lo[kind], bank_[:, :], bias[kind][:, nth:nth + 1], part_hi[kind],
                                             ALU.add, ALU.subtract).then_inc(split_ready, 1)
                if kind == "h":
                    rows = slice(nth * P, (nth + 1) * P)
                    dve.scalar_tensor_tensor(h_lo[:, :, rows], bank_[:, :].rearrange("p (c n) -> p c n", c=C), 0.0,
                                             h_hi[:, :, rows], ALU.max, ALU.subtract).then_inc(split_ready, 1)
                if kind == "m":
                    dve.scalar_tensor_tensor(top_lo[:, :], bank_[0:MAXIMA, 0:P], -1.0, top_hi[:, :],
                                             ALU.mult, ALU.subtract).then_inc(split_ready, 1)
                if kind == "o":
                    dve.wait_ge(work_full, number + 1)
                    dve.wait_ge(res_ready, b_out * T + (nth + 1))
                    dve.tensor_tensor(res[:, nth, :], bank_[:, :], res[:, nth, :], ALU.add).then_inc(out_ready, 1)

            def invert_sums(u, chunk):
                cols = slice(chunk * P, (chunk + 1) * P)
                dve.wait_ge(sum_copied, u + 1)
                dve.reciprocal(recip[:, cols], recip[:, cols]).then_inc(recip_done, 1)

            def normalise(u, g):
                dve.wait_ge(recip_done, u * C + C)
                dve.wait_ge(value_copied, u + 1)
                dve.tensor_tensor(attn[:, g % 2, :], attn[:, g % 2, :], recip[:, :],
                                  ALU.mult).then_inc(attn_scaled, 1)

            def attention_lo(u, g):
                dve.wait_ge(attn_hi_ready, u + 1)
                dve.scalar_tensor_tensor(attn_lo[:, g, :], attn[:, g % 2, :], bias["v"][:, g:g + 1], attn_hi[:, g, :],
                                         ALU.add, ALU.subtract).then_inc(attn_ready, 1)

            def split_weights(names):
                for name in names:
                    n = "qkvo".index(name)
                    dve.wait_ge(w_hi_done, n + 1)
                    dve.tensor_tensor(w_lo[name][:, :, :], probs[:, n % 2, :, :], w_hi[name][:, :, :],
                                      ALU.subtract).then_inc(w_split, 1)

            layernorm_stats(0, (0, 1))
            layernorm_stats(0, (2, 3))
            layernorm_var(0)
            layernorm_apply(0)
            split_weights("q")
            split_weights("k")
            convert_mask(0)
            dve.wait_ge(bias_in, 4 * DMA)
            seen, splits = {}, 0
            for n, kind in enumerate(PROLOGUE):
                nth = seen.get(kind, 0)
                if kind == "w" and not nth:
                    split_weights("vo")
                if kind == "m":
                    maxima(0, 0, 0, 0, 0, MAXIMA)
                evacuate(kind, nth, work[n % 2], n, splits, None)
                seen[kind] = nth + 1
                splits += kind in "hqkm"

            def item(b, g, s, n, kind, nth):
                k, splits = item_number(b, g, s, n)
                group = (g + 2) % 4 if kind in "qk" else nth
                evacuate(kind, group, work_bank(b, g, s, n), work_before(b) + k,
                         splits_before(b) + splits, b - 1)

            for b, phase in batches(dve):
                first = isinstance(b, int) and b == 0
                last = isinstance(b, int) and b == B - 1
                for g in range(4):
                    for s in range(4):
                        u = b * G + g
                        items = slot_items(b, g, s)
                        share = 0 if last and g == 3 else MAX_SHARE[s]
                        at = MAX_FIRST[s]
                        batch_next = b + 1 if g == 3 else b
                        for n, kind, nth in items:
                            if kind == "m":
                                item(b, g, s, n, kind, nth)
                        begun = min(4, share)
                        maxima(u + 1, batch_next, phase, g + 1, at, begun)
                        if s == ATTENTION_SLOT[g] and g != 2 and not (first and g < 2):
                            attention_lo(u - 2, (g - 2) % 4)
                        if not (first and g == 0):
                            for chunk in {0: (), 1: (0,), 2: (1, 2), 3: (3,)}[s]:
                                invert_sums(u - 1, chunk)
                            if s == 3:
                                normalise(u - 1, (g - 1) % 4)
                        if not last:
                            if (g, s) == (0, 1):
                                layernorm_stats(b + 1, (0, 1))
                            if (g, s) == (0, 2):
                                layernorm_stats(b + 1, (2, 3))
                                layernorm_var(b + 1)
                            if (g, s) == (1, 0):
                                layernorm_apply(b + 1)
                            if (g, s) == (2, 3):
                                convert_mask(b + 1)
                        for n, kind, nth in items:
                            if kind in "md":
                                continue
                            item(b, g, s, n, kind, nth)
                            if begun < share:
                                maxima(u + 1, batch_next, phase, g + 1, at + begun, 1)
                                begun += 1
                        maxima(u + 1, batch_next, phase, g + 1, at + begun, share - begun)
                        if s == ATTENTION_SLOT[g] and g == 2:
                            attention_lo(u - 2, (g - 2) % 4)
            attention_lo(B * G - 2, G - 2)
            for chunk in range(C):
                invert_sums(B * G - 1, chunk)
            normalise(B * G - 1, G - 1)
            attention_lo(B * G - 1, G - 1)
            for t in range(T):
                k = len(of_batch[B - 1]) + 1 + t
                evacuate("o", t, bank_number(B - 1, k), work_before(B - 1) + k, None, B - 1)

        @block.tensor
        def _(pe):
            def project(to, pairs, done):
                for n, (lhs, rhs) in enumerate(pairs):
                    mm = pe.matmul(to[:, :], lhs, rhs, start=(n == 0), stop=(n == len(pairs) - 1))
                mm.then_inc(done, 1)

            def do_work(kind, nth, bank_):
                cols = slice(nth * P, (nth + 1) * P)
                if kind in "qk":
                    hi, lo = w_hi[kind], w_lo[kind]
                    project(bank_, [pair for c in range(C) for pair in
                                    ((hi[:, c, cols], h_hi[:, c, :]), (hi[:, c, cols], h_lo[:, c, :]),
                                     (lo[:, c, cols], h_hi[:, c, :]))], work_full)
                if kind in "vw":
                    if kind == "v":
                        cols = slice((nth + 2) * P, (nth + 3) * P)
                    project(bank_, [pair for c in range(C) for pair in
                                    ((h_hi[:, c, cols], w_hi["v"][:, c, :]), (h_hi[:, c, cols], w_lo["v"][:, c, :]),
                                     (h_lo[:, c, cols], w_hi["v"][:, c, :]))], work_full)
                if kind == "o":
                    project(bank_, [pair for c in range(C) for pair in
                                    ((attn_hi[:, c, cols], w_hi["o"][:, c, :]), (attn_hi[:, c, cols], w_lo["o"][:, c, :]),
                                     (attn_lo[:, c, cols], w_hi["o"][:, c, :]))], work_full)
                if kind == "h":
                    for c in range(C):
                        mm = pe.transpose(bank_[:, c * P:(c + 1) * P], x_sb[:, nth, c * P:(c + 1) * P], identf[:, :])
                    mm.then_inc(work_full, 1)
                if kind == "b":
                    tile = bank_[:, 0:S // 2].bitcast(BF16)
                    for t in range(T):
                        mm = pe.transpose(tile[:, t * P:(t + 1) * P], mask_q[:, t, cols], identb[:, :])
                    mm.then_inc(work_full, 1)
                if kind == "m":
                    pe.transpose(bank_[0:MAXIMA, 0:P], top[:, :], identf[:, :]).then_inc(work_full, 1)

            def maxima(u, phase, g, first, count):
                slot = stack_slot(phase, g)
                for n in range(first, first + count):
                    if n == 0:
                        pe.wait_ge(stack_in, (u + 1) * (STACK_DMAS * DMA))
                    wait(pe, max_done, u * MAXIMA + (n + 1 - MAX_BANKS))
                    t, j = n // HG, n % HG
                    pe.matmul(max_bank_of(phase, g, n)[:, :], q_stack[0:3 * DH, slot, j, t * P:(t + 1) * P],
                              k_stack[0:3 * DH, slot, j, :], start=True, stop=True).then_inc(max_full, 1)

            def score(b, g, s, j, slot):
                u = b * G + g
                if j == 0 and s == 0:
                    pe.wait_ge(rows_in, (u + 1) * (2 * DMA))
                if j == 0 and g == 0:
                    pe.wait_ge(mask_k_ready, b * T + (s + 1))
                wait(pe, exp_done, u * SCORES + (s * HG + j - 1))
                to = score_bank[j % 2]
                pe.matmul(to[:, :], identb[:, :], mask_k[:, s, :], start=True, stop=False)
                pe.matmul(to[:, :], k_stack[0:3 * DH + 2, slot, j, s * P:(s + 1) * P],
                          q_stack[0:3 * DH + 2, slot, j, :], start=False, stop=True).then_inc(score_full, 1)

            def values(b, g, s):
                u = b * G + g
                pe.wait_ge(exp_done, u * SCORES + (s * HG + HG))
                if g == 0:
                    pe.wait_ge(v_ready, b * T + (s + 1))
                if s == 0:
                    wait(pe, value_copied, u)
                for j in range(HG):
                    h = g * HG + j
                    mm = pe.matmul(value_bank[DH * j:DH * (j + 1), :], v_sb[:, s, h * DH:(h + 1) * DH],
                                   probs[:, s % 2, j, :], start=(s == 0), stop=(s == T - 1))
                mm.then_inc(value_done, 1)

            def sums(u, to):
                pe.wait_ge(add_done, u * ADDS + ADDS)
                for j in range(HG):
                    mm = pe.matmul(to[DH * j:DH * (j + 1), :], ones[:, :], prob_sum[:, j, :],
                                   start=True, stop=True)
                mm.then_inc(work_full, 1)

            emptied = {"v": v_ready, "w": v_ready, "b": mask_k_ready, "o": out_ready, "d": sum_copied}

            def wait_bank(b, k):
                items = items_of(b)
                if k < 2:
                    pe.wait_ge(mask_k_ready, b * T + (T - 1 + k))
                    return
                _, _, kind, nth = items[k - 2]
                if kind == "d":
                    pe.wait_ge(sum_copied, b * G + items[k - 2][0])
                    return
                if kind in emptied:
                    before = {"v": b * T + 2, "w": b * T + T, "b": b * T + T, "o": b * T - T}[kind]
                    pe.wait_ge(emptied[kind], before + (nth + 1))
                else:
                    done = sum(it[2] in "hqkm" for it in items[:k - 2]) + 1
                    pe.wait_ge(split_ready, splits_before(b) + done)

            def run_item(b, g, s, n, kind, nth):
                k, _ = item_number(b, g, s, n)
                wait_bank(b, k)
                u = b * G + g
                if kind == "h":
                    pe.wait_ge(ln_step, b * LN_STEPS + 2 * LN_STEPS)
                if kind == "q" and g == 2:
                    done = max(i for i, it in enumerate(items_of(b)) if it[2] == "h") + 1
                    pe.wait_ge(split_ready, splits_before(b) + sum(it[2] in "hqkm" for it in items_of(b)[:done]))
                if kind == "b":
                    pe.wait_ge(mask_ready, b * T + 2 * T)
                if kind == "m":
                    pe.wait_ge(max_done, u * MAXIMA + 2 * MAXIMA)
                if kind == "o":
                    pe.wait_ge(attn_ready, b * G)
                if kind == "d":
                    sums(u - 1, work_bank(b, g, s, n))
                    return
                group = (g + 2) % 4 if kind in "qk" else nth
                do_work(kind, 0 if kind == "m" else group, work_bank(b, g, s, n))

            pe.wait_ge(consts, CONSTS)
            seen = {}
            for n, kind in enumerate(PROLOGUE):
                nth = seen.get(kind, 0)
                if n >= 2:
                    prev = PROLOGUE[n - 2]
                    count = sum(k in "hqkm" if prev in "hqkm" else k == prev for k in PROLOGUE[:n - 1])
                    pe.wait_ge(emptied.get(prev, split_ready), count)
                if kind == "h":
                    pe.wait_ge(ln_step, LN_STEPS)
                if kind in "qk":
                    pe.wait_ge(split_ready, T)
                    pe.wait_ge(w_split, 1 if kind == "q" else 2)
                if kind == "b":
                    pe.wait_ge(mask_ready, T)
                if kind == "w":
                    pe.wait_ge(w_split, 3)
                if kind == "m":
                    maxima(0, 0, 0, 0, MAXIMA)
                    pe.wait_ge(max_done, MAXIMA)
                do_work(kind, 0 if kind == "m" else nth, work[n % 2])
                seen[kind] = nth + 1
            pe.wait_ge(w_split, 4)

            for b, phase in batches(pe):
                first = isinstance(b, int) and b == 0
                last = isinstance(b, int) and b == B - 1
                for g in range(4):
                    u = b * G + g
                    for s in range(4):
                        items = slot_items(b, g, s)
                        share = 0 if last and g == 3 else MAX_SHARE[s]
                        at = MAX_FIRST[s]
                        begun = 0
                        for j in range(HG):
                            score(b, g, s, j, stack_slot(phase, g))
                            if j == M_AFTER:
                                for n, kind, nth in items:
                                    if kind == "m":
                                        run_item(b, g, s, n, kind, nth)
                            if begun < share:
                                maxima(u + 1, phase, g + 1, at + begun, 1)
                                begun += 1
                        for n, kind, nth in items:
                            if kind in "md":
                                continue
                            run_item(b, g, s, n, kind, nth)
                            if begun < share:
                                maxima(u + 1, phase, g + 1, at + begun, 1)
                                begun += 1
                        maxima(u + 1, phase, g + 1, at + begun, share - begun)
                        if s > 0:
                            values(b, g, s - 1)
                        elif not (first and g == 0):
                            values(b if g > 0 else b - 1, (g - 1) % 4, T - 1)
                            run_item(b, g, s, *items[-1])
            values(B - 1, G - 1, T - 1)
            k = len(of_batch[B - 1])
            pe.wait_ge(out_ready, (B - 1) * T)
            sums(B * G - 1, bank_number(B - 1, k))
            pe.wait_ge(attn_ready, B * G)
            pe.wait_ge(sum_copied, B * G)
            for t in range(T):
                if t >= 2:
                    pe.wait_ge(out_ready, (B - 1) * T + (t - 1))
                do_work("o", t, bank_number(B - 1, k + 1 + t))


_INS = ["x", "adj", "L0_gnn_Wq", "L0_gnn_bq", "L0_gnn_Wk", "L0_gnn_bk", "L0_gnn_Wv", "L0_gnn_bv",
        "L0_gnn_Wo", "L0_gnn_bo"]


def kernel(**inputs):
    import numpy as _np
    import concourse.bacc as _bacc
    from concourse import mybir as _mybir
    from concourse.bass_utils import run_bass_kernel_spmd as _run

    nc = _bacc.Bacc("TRN2", target_bir_lowering=False, num_devices=1, dynamic_dma_scratch_size=1024)
    arrays, args = {}, []
    for name in _INS:
        a = _np.ascontiguousarray(inputs[name])
        arrays[f"in_{name}_dram"] = a
        args.append(nc.dram_tensor(f"in_{name}_dram", a.shape, _mybir.dt.from_np(a.dtype), kind="ExternalInput").ap())
    shape = inputs["x"].shape
    args.append(nc.dram_tensor("out_0_dram", shape, _mybir.dt.float32, kind="ExternalOutput").ap())
    build_kernel(nc, *args)
    r = _run(nc, [arrays], core_ids=[0])
    return r.results[0]["out_0_dram"]
```

```python
from contextlib import ExitStack

import concourse.bass as bass
from concourse import mybir

ALU = mybir.AluOpType
ACT = mybir.ActivationFunctionType
F32 = mybir.dt.float32
F32R = mybir.dt.float32r
BF16 = mybir.dt.bfloat16
I32 = mybir.dt.int32

P = 128
HEADS = 16
DH = 32
HG = P // DH
STACK_SLOTS = 3
MASKED = -(2.0 ** 100)
MASKED_EXP = 2.0
NEG_MAX = -3.0e38
EPS = 1e-5
DMA = 16

WORK = {(g, s): [] for g in range(4) for s in range(4)}
for _g in range(4):
    WORK[_g, 0] += ["q"]
    WORK[_g, 1] += ["k"]
    WORK[_g, 2] += [["v"], ["o"], ["o"], ["w"]][_g]
    WORK[_g, 3] += ["m"]
WORK[0, 3] += ["v"]
WORK[1, 1] += ["h"]
WORK[1, 2] += ["h", "h"]
WORK[1, 3] += ["h", "o"]
WORK[2, 3] += ["o"]
WORK[3, 1] += ["b"]
WORK[3, 2] += ["b"]
WORK[3, 3] += ["w", "b", "b"]
for _g in range(4):
    WORK[_g, 0] += ["d"]
PROLOGUE = list("hhhhqkbbqkwwmbb")
MAX_SHARE = [6, 6, 4, 0]
MAX_FIRST = [0, 6, 12, 16]
MAX_BANKS = 3
PARTS = 3
PROLOGUE_MAXIMA = {10: range(3), 11: range(3, 8), 12: range(8, 16)}
MASKED_LATER = [(1, 2, 3), (3,), (2, 3), (1, 2, 3)]


def batch_work(first, last):
    items, seen = [], {}
    for g in range(4):
        for s in range(4):
            for kind in WORK[g, s]:
                if first and (kind == "o" or (kind == "d" and g == 0)):
                    continue
                if last and (kind in "hbw" or (kind in "qk" and g >= 2) or (kind == "m" and g == 3)):
                    continue
                items.append((g, s, kind, seen.get(kind, 0)))
                seen[kind] = seen.get(kind, 0) + 1
    return items


def steps_of(items, s):
    light = [it for it in items if it[1] == "m"]
    rest = [it for it in items if it[1] not in "md"]
    products = list(range(MAX_FIRST[s], MAX_FIRST[s] + MAX_SHARE[s]))

    def product():
        return [("max", products.pop(0))] if products else []

    def whole(it):
        return [("part", (it, part)) for part in range(PARTS)] + [("hi", it), ("lo", it)]

    parts = range(PARTS)
    steps = []
    if s == 0 and rest:
        steps = [("part", (rest[0], 0))] + product()
        parts = range(1, PARTS)
    steps += [("score", 0)] + [step for it in light for step in whole(it)] + product()
    steps += [("score", 1)] + product()
    while rest and rest[0][1] == "h":
        steps += whole(rest.pop(0))
    steps += [("side", 0)] + [("mask", j) for j in MASKED_LATER[s] if j < 2]
    lo = []
    if rest:
        it = rest.pop(0)
        for part in parts:
            steps += [("part", (it, part))] + (product() if part < PARTS - 1 else [])
        steps += [("hi", it)]
        lo = [("lo", it)]
    steps += [("score", 2)] + product() + lo + [("score", 3)] + product()
    steps += [("sums", 0)]
    steps += [("mask", j) for j in MASKED_LATER[s] if j >= 2]
    while rest:
        steps += whole(rest.pop(0)) + product()
    while products:
        steps += product()
    return steps


def build_kernel(nc, x, adj, Wq, bq, Wk, bk, Wv, bv, Wo, bo, out):
    B, S, D = x.shape
    T = S // P
    C = D // P
    G = HEADS // HG
    assert T == 4 and C == 4 and G == 4 and D == HEADS * DH and (B - 4) % 3 == 0
    TURNS = (B - 4) // 3
    SCALE = float(DH) ** -0.5
    MAXIMA = HG * T
    SCORES = HG * T
    ADDS = HG * (T - 1)
    LATER = sum(map(len, MASKED_LATER))
    STACK_DMAS = 12
    SPLITS = 16
    LN_STEPS = 3 * T + 1
    CONSTS = 7

    plain = batch_work(False, False)
    of_batch = {0: batch_work(True, False), B - 1: batch_work(False, True)}
    assert len(plain) % 2 == 0

    def items_of(b):
        return of_batch.get(b, plain) if isinstance(b, int) else plain

    def work_before(b):
        if isinstance(b, int) and b == 0:
            return len(PROLOGUE)
        return b * len(plain) + (len(PROLOGUE) + len(of_batch[0]) - len(plain))

    def splits_before(b):
        return b * SPLITS + sum(k in "hqkm" for k in PROLOGUE)

    def item_number(b, g, s, n):
        items = items_of(b)
        k = [i for i, it in enumerate(items) if it[:2] == (g, s)][n]
        split = sum(it[2] in "hqkm" for it in items[:k])
        return k, split

    def slot_items(b, g, s):
        return [(n, it[2], it[3]) for n, it in
                enumerate(it for it in items_of(b) if it[:2] == (g, s))]

    with ExitStack() as ctx:
        def sb(name, shape, dt):
            return ctx.enter_context(nc.sbuf_tensor(name, shape, dt))

        def bank(name):
            return ctx.enter_context(nc.psum_tensor(name, [P, 512], F32))

        def sem(name):
            return ctx.enter_context(nc.semaphore(name))

        w_hi = {n: sb(f"w{n}_hi", [P, C, D], F32R) for n in "qkvo"}
        w_lo = {n: sb(f"w{n}_lo", [P, C, D], F32R) for n in "qkvo"}
        stacks = sb("stacks", [P, STACK_SLOTS, 2, HG, S], F32R)
        k_stack, q_stack = stacks[:, :, 0, :, :], stacks[:, :, 1, :, :]
        parts = sb("parts", [P, 4, S], F32R)
        part_hi = {"k": parts[:, 0, :], "q": parts[:, 2, :]}
        part_lo = {"k": parts[:, 1, :], "q": parts[:, 3, :]}
        probs = sb("probs", [P, 2, HG, S], F32)
        prob_sum = sb("prob_sum", [P, HG, S], F32)
        h_hi = sb("h_hi", [P, C, S], F32R)
        h_lo = sb("h_lo", [P, C, S], F32R)
        v_sb = sb("v_sb", [P, T, D], F32)
        x_sb = sb("x_sb", [P, T, D], F32)
        mask_q = sb("mask_q", [P, T, S], BF16)
        mask_k = sb("mask_k", [P, T, S], BF16)
        attn_hi = sb("attn_hi", [P, G, S], F32R)
        attn_lo = sb("attn_lo", [P, G, S], F32R)
        attn = sb("attn", [P, 2, S], F32)
        recip = sb("recip", [P, S], F32)
        newton = sb("newton", [P, S], F32)
        res = sb("res", [P, T, D], F32)
        bo_all = sb("bo_all", [P, D], F32)
        bias = {n: sb(f"bias_{n}", [P, G], F32) for n in "qkv"}
        identb = sb("identb", [P, P], BF16)
        identf = sb("identf", [P, P], F32)
        ones = sb("ones", [P, DH], F32)
        top = sb("top", [P, MAXIMA], F32)
        top_hi = sb("top_hi", [MAXIMA, P], F32R)
        top_lo = sb("top_lo", [MAXIMA, P], F32R)
        stats = sb("stats", [P, T, 6], F32)
        moments = sb("moments", [P, T, 2], F32)
        var_eps = sb("var_eps", [P, T], F32)
        rstd = sb("rstd", [P, T], F32)
        minus_half = sb("minus_half", [P, T], F32)

        work = [bank("work0"), bank("work1")]
        max_bank = [bank(f"max{n}") for n in range(MAX_BANKS)]
        score_bank = [bank("score0"), bank("score1")]
        value_bank = bank("value")

        x_in, adj_in, bias_in, res_in = map(sem, ["x_in", "adj_in", "bias_in", "res_in"])
        w_in = [sem("w_in0"), sem("w_in1")]
        stack_in, rows_in, out_stored = map(sem, ["stack_in", "rows_in", "out_stored"])
        consts, w_hi_done, w_split = map(sem, ["consts", "w_hi_done", "w_split"])
        ln_step, rstd_ready, mask_ready, res_ready = map(sem, ["ln_step", "rstd_ready", "mask_ready", "res_ready"])
        work_full, hi_ready, split_ready = map(sem, ["work_full", "hi_ready", "split_ready"])
        v_ready, mask_k_ready, out_ready = map(sem, ["v_ready", "mask_k_ready", "out_ready"])
        passed = sem("passed")
        max_full, max_done = map(sem, ["max_full", "max_done"])
        score_full, exp_done, value_done = map(sem, ["score_full", "exp_done", "value_done"])
        add_done, later_masked = map(sem, ["add_done", "later_masked"])
        sum_copied, log_done, recip_ready = map(sem, ["sum_copied", "log_done", "recip_ready"])
        reciprocal_checked, newton_ready = map(sem, ["reciprocal_checked", "newton_ready"])
        value_copied, attn_scaled, attn_biased, attn_hi_ready, attn_ready = map(
            sem, ["value_copied", "attn_scaled", "attn_biased", "attn_hi_ready", "attn_ready"])

        def wait(eng, s, value):
            if not (isinstance(value, int) and value <= 0):
                eng.wait_ge(s, value)

        def wait_alone(eng, s, value):
            eng.wait_ge(s, value)
            eng.sem_inc(passed, 1)

        def later_count(u, s, j):
            return u * LATER + (sum(map(len, MASKED_LATER[:s])) + MASKED_LATER[s].index(j) + 1)

        def batches(eng):
            yield 0, 0
            with eng.Fori(0, TURNS) as i:
                for r in range(3):
                    yield i * 3 + (1 + r), (1 + r) % 3
            for b in range(1 + 3 * TURNS, B):
                yield b, b % 3

        def stack_slot(phase, g):
            return (phase + g) % STACK_SLOTS

        def max_bank_of(phase, g, n):
            return max_bank[(phase + g + n) % MAX_BANKS]

        def work_bank(b, g, s, n):
            return bank_number(b, item_number(b, g, s, n)[0])

        def bank_number(b, k):
            before = len(PROLOGUE) + (0 if isinstance(b, int) and b == 0 else len(of_batch[0]))
            return work[(before + k) % 2]

        last_banks = max_bank + [bank_number(B - 1, len(of_batch[B - 1]) + 1)]

        def adj_sb(b):
            return (res if isinstance(b, int) and b == 0 else x_sb)[:, :, :].bitcast(I32)

        def staged(name):
            return res[:, :, :] if name == "o" else probs[:, int(name == "k"), :, :]

        block = ctx.enter_context(nc.Block())

        @block.sync
        def _(sp):
            def load_rows(b):
                for t in range(T):
                    sp.dma_start(x_sb[:, t, :], x[b, t * P:(t + 1) * P, :]).then_inc(x_in, DMA)

            def load_adj(b):
                for t in range(T):
                    sp.dma_start(adj_sb(b)[:, t, :], adj[b, t * P:(t + 1) * P, :]).then_inc(adj_in, DMA)

            def load_residual(b):
                for t in range(T):
                    sp.dma_start(res[:, t, :], x[b, t * P:(t + 1) * P, :]).then_inc(res_in, DMA)

            def store(b, t):
                sp.wait_ge(out_ready, b * T + (t + 1))
                sp.dma_start(out[b, t * P:(t + 1) * P, :], res[:, t, :]).then_inc(out_stored, DMA)

            def stack(slot, count):
                sp.wait_ge(split_ready, count)
                for r, pair in enumerate((slice(0, 3, 2), slice(0, 4, 3), slice(1, 3))):
                    for j in range(HG):
                        sp.dma_start(stacks[DH * r:DH * (r + 1), slot, :, j, :].bitcast(F32),
                                     parts[DH * j:DH * (j + 1), pair, :].bitcast(F32)).then_inc(stack_in, DMA)

            def maxima_rows(slot, count):
                sp.wait_ge(split_ready, count)
                for r, src in enumerate((top_hi, top_lo)):
                    row = 3 * DH + r
                    sp.dma_start(q_stack[row:row + 1, slot, :, :].bitcast(F32),
                                 src[:, :].bitcast(F32)).then_inc(rows_in, DMA)

            load_rows(0)
            for n, w in enumerate((Wq, Wk)):
                sp.dma_start(staged("qk"[n]), w.rearrange("(c p) n -> p c n", p=P)).then_inc(w_in[n], DMA)
            for n, v in (("q", bq), ("k", bk), ("v", bv)):
                sp.dma_start(bias[n][:, :], v.rearrange("(g p) -> p g", p=P),
                             allow_slow_non_contiguous=True).then_inc(bias_in, DMA)
            sp.dma_start(bo_all[:, :], bass.AP(tensor=bo.tensor, offset=bo.offset,
                                               ap=[[0, P], [1, D]])).then_inc(bias_in, DMA)
            load_adj(0)
            sp.wait_ge(w_split, 1)
            sp.dma_start(staged("v"), Wv.rearrange("(c p) n -> p c n", p=P)).then_inc(w_in[0], DMA)
            count = 0
            for n, kind in enumerate(PROLOGUE):
                count += kind in "hqkm"
                if kind == "k":
                    stack(PROLOGUE[:n].count("k"), count)
                    if n == PROLOGUE.index("k"):
                        sp.wait_ge(mask_ready, T)
                        sp.dma_start(staged("o"), Wo.rearrange("(c p) n -> p c n", p=P)).then_inc(w_in[1], DMA)
                if kind == "m":
                    maxima_rows(0, count)

            for b, phase in batches(sp):
                last = isinstance(b, int) and b == B - 1
                first = isinstance(b, int) and b == 0
                for g in range(4):
                    for s in range(4):
                        for n, kind, _ in slot_items(b, g, s):
                            count = splits_before(b) + item_number(b, g, s, n)[1] + 1
                            if kind == "k":
                                stack(stack_slot(phase, g + 2), count)
                            if kind == "m":
                                maxima_rows(stack_slot(phase, g + 1), count)
                        if (g, s) == (0, 0) and not last:
                            if first:
                                sp.wait_ge(work_full, T)
                            else:
                                sp.wait_ge(mask_ready, b * T + T)
                            load_rows(b + 1)
                        if (g, s) == (0, 3) and first:
                            sp.wait_ge(w_split, 4)
                            sp.sem_inc(out_stored, T * DMA)
                        if (g, s) == (0, 3) and not first:
                            sp.wait_ge(out_stored, b * (T * DMA))
                            load_residual(b - 1)
                        if not first:
                            for n, kind, nth in slot_items(b, g, s):
                                if kind == "o":
                                    store(b - 1, nth)
                        if (g, s) == (1, 3) and not last:
                            k = max(i for i, it in enumerate(items_of(b)) if it[2] == "h")
                            sp.wait_ge(work_full, work_before(b) + (k + 1))
                            load_adj(b + 1)
            sp.wait_ge(out_stored, B * T * DMA)
            load_residual(B - 1)
            for t in range(T):
                store(B - 1, t)
            sp.wait_ge(out_stored, (B + 1) * T * DMA)

        @block.gpsimd
        def _(pool):
            pool.memset(identb[:, :], 0.0).then_inc(consts, 1)
            pool.memset(identf[:, :], 0.0).then_inc(consts, 1)
            pool.wait_ge(consts, 2)
            for ident in (identb, identf):
                pool.affine_select(out=ident[:, :], in_=ident[:, :], compare_op=ALU.not_equal, fill=1.0,
                                   base=0, pattern=[[-1, P]], channel_multiplier=1).then_inc(consts, 1)
            pool.memset(ones[:, :], 1.0).then_inc(consts, 1)
            pool.memset(minus_half[:, :], -0.5).then_inc(consts, 1)
            pool.wait_ge(consts, CONSTS - 1)
            pool.memset(stacks[3 * DH:P, :, 0, :, :].bitcast(F32), 1.0).then_inc(consts, 1)
            pool.wait_ge(consts, CONSTS)

            def reciprocal_std(b):
                pool.wait_ge(ln_step, b * LN_STEPS + (2 * T + 1))
                pool.tensor_tensor(rstd[:, :], var_eps[:, :], minus_half[:, :], ALU.pow).then_inc(rstd_ready, 1)

            def add_output_bias(b, tiles):
                pool.wait_ge(bias_in, 4 * DMA)
                pool.wait_ge(res_in, b * (T * DMA) + T * DMA)
                for t in tiles:
                    pool.tensor_tensor(res[:, t, :], res[:, t, :], bo_all[:, :], ALU.add).then_inc(res_ready, 1)

            def normalise(u, g):
                pool.wait_ge(newton_ready, u + 1)
                pool.tensor_tensor(attn[:, g % 2, :], newton[:, :], recip[:, :], ALU.mult).then_inc(attn_scaled, 1)

            def attention_lo(u, g):
                pool.wait_ge(attn_hi_ready, u + 1)
                pool.tensor_tensor(attn_lo[:, g, :], attn[:, g % 2, :], attn_hi[:, g, :],
                                   ALU.subtract).then_inc(attn_ready, 1)

            def add_tiles(b, g, s, b_next):
                u = b * G + g
                for j in range(HG):
                    pool.wait_ge(exp_done, u * SCORES + (s * HG + j + 1))
                    read = [tile for tile in ((0, 1) if s == 1 else (s,)) if j in MASKED_LATER[tile]]
                    if read:
                        pool.wait_ge(later_masked, later_count(u, read[-1], j))
                    if s == 1:
                        wait(pool, sum_copied, u)
                        pool.tensor_tensor(prob_sum[:, j, :], probs[:, 0, j, :], probs[:, 1, j, :],
                                           ALU.add).then_inc(add_done, 1)
                    else:
                        if (g, s, j) == (0, 3, 2) and b_next is not None:
                            reciprocal_std(b_next)
                        pool.wait_ge(add_done, u * ADDS + ((s - 2) * HG + j + 1))
                        pool.tensor_tensor(prob_sum[:, j, :], prob_sum[:, j, :], probs[:, s % 2, j, :],
                                           ALU.add).then_inc(add_done, 1)

            reciprocal_std(0)
            for b, _ in batches(pool):
                last = isinstance(b, int) and b == B - 1
                first = isinstance(b, int) and b == 0
                for g in range(4):
                    u = b * G + g
                    if g == 3:
                        attention_lo(u - 3, 0)
                    if not (first and g < 2):
                        normalise(u - 2, (g - 2) % 4)
                        if g != 2:
                            attention_lo(u - 2, (g - 2) % 4)
                    if g == 1 and not first:
                        add_output_bias(b - 1, (0, 1))
                    for s in range(1, 4):
                        add_tiles(b, g, s, None if last else b + 1)
                        if (g, s) == (1, 1) and not first:
                            add_output_bias(b - 1, (2, 3))
            normalise(B * G - 2, G - 2)
            attention_lo(B * G - 2, G - 2)
            normalise(B * G - 1, G - 1)
            attention_lo(B * G - 1, G - 1)

        @block.scalar
        def _(act):
            act.preload_act_table_set("natural_log_exp_and_others")

            def weights_hi(name):
                n = "qkvo".index(name)
                act.wait_ge(w_in[n % 2], DMA * (n // 2 + 1))
                act.copy(w_hi[name][:, :, :], staged(name)).then_inc(w_hi_done, 1)

            weights_hi("q")
            weights_hi("k")

            def evacuate(kind, nth, bank_, number, stacked):
                if kind == "o":
                    return
                act.wait_ge(work_full, number + 1)
                if kind in "qk":
                    wait(act, stack_in, stacked)
                    act.activation(part_hi[kind], bank_[:, :], ACT.Identity,
                                   bias=bias[kind][:, nth:nth + 1]).then_inc(hi_ready, 1)
                if kind == "h":
                    act.activation(h_hi[:, :, nth * P:(nth + 1) * P],
                                   bank_[:, :].rearrange("p (c n) -> p c n", c=C), ACT.Relu).then_inc(hi_ready, 1)
                if kind == "m":
                    wait(act, rows_in, stacked)
                    act.activation(top_hi[:, :], bank_[0:MAXIMA, 0:P], ACT.Copy, scale=-1.0).then_inc(hi_ready, 1)
                if kind in "vw":
                    tile = nth + (2 if kind == "v" else 0)
                    act.copy(v_sb[:, tile, :], bank_[:, :]).then_inc(v_ready, 1)
                if kind == "d":
                    wait(act, attn_scaled, stacked)
                    act.copy(newton[:, :], bank_[:, :]).then_inc(sum_copied, 1)
                    act.wait_ge(sum_copied, stacked + 1)
                    act.activation(recip[:, :], newton[:, :], ACT.Ln).then_inc(log_done, 1)
                    act.wait_ge(log_done, stacked + 1)
                    act.activation(recip[:, :], recip[:, :], ACT.Exp, scale=-1.0).then_inc(recip_ready, 1)
                if kind == "b":
                    if stacked is not None:
                        act.wait_ge(later_masked, later_count(stacked, nth, MASKED_LATER[nth][-1]))
                    act.activation(mask_k[:, nth, :], bank_[:, 0:S // 2].bitcast(BF16), ACT.Copy,
                                   scale=MASKED_EXP).then_inc(mask_k_ready, 1)

            seen = {}
            for n, kind in enumerate(PROLOGUE):
                nth = seen.get(kind, 0)
                stacked = nth * STACK_DMAS * DMA if kind in "qk" else None if kind == "b" else 0
                if n == PROLOGUE.index("q"):
                    act.wait_ge(bias_in, 4 * DMA)
                if n == PROLOGUE.index("w"):
                    weights_hi("v")
                evacuate(kind, nth, work[n % 2], n, stacked)
                seen[kind] = nth + 1
                if kind == "m":
                    weights_hi("o")

            def exponential(b, g, s, j):
                u = b * G + g
                if j == 0:
                    wait(act, value_done, u * T + (s - 1))
                wait(act, add_done, u * ADDS + {0: 5 + j - ADDS, 1: 9 + j - ADDS, 2: j + 1, 3: j + 1}[s])
                act.wait_ge(score_full, u * SCORES + (s * HG + j + 1))
                act.activation(probs[:, s % 2, j, :], score_bank[j % 2][:, :], ACT.Exp,
                               scale=SCALE).then_inc(exp_done, 1)

            def copy_values(u, g):
                act.wait_ge(value_done, u * T + T)
                wait(act, attn_ready, u - 1)
                act.activation(attn[:, g % 2, :], value_bank[:, :], ACT.Copy, scale=-1.0).then_inc(value_copied, 1)

            def attention_hi(u, g):
                act.wait_ge(attn_scaled, u + 1)
                act.activation(attn[:, g % 2, :], attn[:, g % 2, :], ACT.Identity,
                               bias=bias["v"][:, g:g + 1]).then_inc(attn_biased, 1)
                act.wait_ge(attn_biased, u + 1)
                act.copy(attn_hi[:, g, :], attn[:, g % 2, :]).then_inc(attn_hi_ready, 1)

            def item(b, g, s, n, kind, nth):
                u = b * G + g
                k, _ = item_number(b, g, s, n)
                group = (g + 2) % 4 if kind in "qk" else nth
                free = {"q": (u + 2) * (STACK_DMAS * DMA), "k": (u + 2) * (STACK_DMAS * DMA),
                        "m": (u + 1) * (2 * DMA), "d": u - 1, "b": u}.get(kind)
                evacuate(kind, group, work_bank(b, g, s, n), work_before(b) + k, free)

            for b, _ in batches(act):
                first = isinstance(b, int) and b == 0
                for g in range(4):
                    for s in range(4):
                        u = b * G + g
                        items = slot_items(b, g, s)
                        for step, what in steps_of(items, s):
                            if step == "score":
                                exponential(b, g, s, what)
                                if (s, what) == (1, 0) and not (first and g == 0):
                                    copy_values(u - 1, (g - 1) % 4)
                                    sums_item = slot_items(b, g, 0)[-1]
                                    item(b, g, 0, *sums_item)
                            if step == "hi":
                                item(b, g, s, *what)
                        if s == 0 and g != 2 and not (first and g < 2):
                            attention_hi(u - 2, (g - 2) % 4)
                        if (g, s) == (2, 3):
                            if not first:
                                k = max(i for i, it in enumerate(items_of(b)) if it[2] == "o")
                                act.wait_ge(work_full, work_before(b) + (k + 1))
                            attention_hi(u - 2, (g - 2) % 4)
            attention_hi(B * G - 2, G - 2)
            copy_values(B * G - 1, G - 1)
            k = len(of_batch[B - 1])
            evacuate("d", 0, bank_number(B - 1, k), work_before(B - 1) + k, B * G - 1)
            attention_hi(B * G - 1, G - 1)

        @block.vector
        def _(dve):
            def layernorm_stats(b, tiles):
                dve.wait_ge(x_in, b * (T * DMA) + T * DMA)
                for t in tiles:
                    dve.bn_stats(stats[:, t, :], x_sb[:, t, :]).then_inc(ln_step, 1)
                wait_alone(dve, ln_step, b * LN_STEPS + (2 * tiles[0] + 2))
                for t in tiles:
                    dve.bn_aggr(moments[:, t, :], stats[:, t, :]).then_inc(ln_step, 1)

            def layernorm_var(b):
                dve.wait_ge(ln_step, b * LN_STEPS + 2 * T)
                wait(dve, rstd_ready, b)
                dve.tensor_scalar(var_eps[:, :], moments[:, :, 1], EPS, None, ALU.add).then_inc(ln_step, 1)

            def layernorm_apply(b):
                dve.wait_ge(rstd_ready, b + 1)
                for t in range(T):
                    dve.tensor_scalar(x_sb[:, t, :], x_sb[:, t, :], moments[:, t, 0:1], rstd[:, t:t + 1],
                                      ALU.subtract, ALU.mult).then_inc(ln_step, 1)

            def convert_mask(b):
                dve.wait_ge(adj_in, b * (T * DMA) + T * DMA)
                wait(dve, max_done, b * (G * MAXIMA))
                wait(dve, work_full, 0 if isinstance(b, int) and b == 0 else work_before(b - 1))
                for t in range(T):
                    dve.tensor_scalar(mask_q[:, t, :], adj_sb(b)[:, t, :], 0, MASKED, ALU.is_equal,
                                      ALU.mult).then_inc(mask_ready, 1)

            def maximum(u, batch_next, phase, g, n):
                if n == 0:
                    dve.wait_ge(mask_ready, batch_next * T + T)
                wait_alone(dve, max_full, u * MAXIMA + (n + 1))
                t, j = n // HG, n % HG
                scores = max_bank_of(phase, g, n)
                dve.tensor_tensor_reduce(scores[:, :], scores[:, :], mask_q[:, t, :],
                                         1.0, NEG_MAX, ALU.add, ALU.max,
                                         top[:, j * T + t:j * T + t + 1]).then_inc(max_done, 1)

            def evacuate(kind, nth, bank_, number, splits, b_out):
                if kind in "qkhm":
                    dve.wait_ge(hi_ready, splits + 1)
                if kind in "qk":
                    dve.scalar_tensor_tensor(part_lo[kind], bank_[:, :], bias[kind][:, nth:nth + 1], part_hi[kind],
                                             ALU.add, ALU.subtract).then_inc(split_ready, 1)
                if kind == "h":
                    rows = slice(nth * P, (nth + 1) * P)
                    dve.scalar_tensor_tensor(h_lo[:, :, rows], bank_[:, :].rearrange("p (c n) -> p c n", c=C), 0.0,
                                             h_hi[:, :, rows], ALU.max, ALU.subtract).then_inc(split_ready, 1)
                if kind == "m":
                    dve.scalar_tensor_tensor(top_lo[:, :], bank_[0:MAXIMA, 0:P], -1.0, top_hi[:, :],
                                             ALU.mult, ALU.subtract).then_inc(split_ready, 1)
                if kind == "o":
                    dve.wait_ge(work_full, number + 1)
                    dve.wait_ge(res_ready, b_out * T + (nth + 1))
                    dve.tensor_tensor(res[:, nth, :], bank_[:, :], res[:, nth, :], ALU.add).then_inc(out_ready, 1)

            def check_reciprocal(u):
                dve.wait_ge(recip_ready, u + 1)
                dve.tensor_tensor(newton[:, :], newton[:, :], recip[:, :], ALU.mult).then_inc(reciprocal_checked, 1)

            def correct(u, g):
                dve.wait_ge(value_copied, u + 1)
                dve.wait_ge(reciprocal_checked, u + 1)
                dve.scalar_tensor_tensor(newton[:, :], newton[:, :], -2.0, attn[:, g % 2, :],
                                         ALU.add, ALU.mult).then_inc(newton_ready, 1)

            def mask_later(b, g, s, j):
                dve.wait_ge(exp_done, (b * G + g) * SCORES + (s * HG + j + 1))
                dve.scalar_tensor_tensor(probs[:, s % 2, j, :], mask_k[:, s, :], -MASKED_EXP * MASKED,
                                         probs[:, s % 2, j, :], ALU.add, ALU.min).then_inc(later_masked, 1)

            def split_weights(names):
                for name in names:
                    n = "qkvo".index(name)
                    dve.wait_ge(w_hi_done, n + 1)
                    dve.tensor_tensor(w_lo[name][:, :, :], staged(name), w_hi[name][:, :, :],
                                      ALU.subtract).then_inc(w_split, 1)

            layernorm_stats(0, (0, 1))
            layernorm_stats(0, (2, 3))
            layernorm_var(0)
            layernorm_apply(0)
            split_weights("q")
            seen, splits = {}, 0
            for n, kind in enumerate(PROLOGUE):
                nth = seen.get(kind, 0)
                if n == PROLOGUE.index("q"):
                    split_weights("k")
                    convert_mask(0)
                    dve.wait_ge(bias_in, 4 * DMA)
                if kind == "w" and not nth:
                    split_weights("v")
                for product in PROLOGUE_MAXIMA.get(n, ()):
                    maximum(0, 0, 0, 0, product)
                evacuate(kind, nth, work[n % 2], n, splits, None)
                if kind == "m":
                    split_weights("o")
                seen[kind] = nth + 1
                splits += kind in "hqkm"

            def item(b, g, s, n, kind, nth):
                k, splits = item_number(b, g, s, n)
                group = (g + 2) % 4 if kind in "qk" else nth
                evacuate(kind, group, work_bank(b, g, s, n), work_before(b) + k,
                         splits_before(b) + splits, b - 1)

            def aside(b, g, s, first, last):
                u = b * G + g
                if not (first and g == 0):
                    if s == 3:
                        correct(u - 1, (g - 1) % 4)
                if not last:
                    if (g, s) == (0, 2):
                        layernorm_stats(b + 1, (0, 1))
                    if (g, s) == (0, 3):
                        layernorm_stats(b + 1, (2, 3))
                        layernorm_var(b + 1)
                    if (g, s) == (2, 3):
                        convert_mask(b + 1)

            for b, phase in batches(dve):
                first = isinstance(b, int) and b == 0
                last = isinstance(b, int) and b == B - 1
                for g in range(4):
                    for s in range(4):
                        u = b * G + g
                        items = slot_items(b, g, s)
                        batch_next = b + 1 if g == 3 else b
                        for step, what in steps_of(items, s):
                            if step == "lo":
                                item(b, g, s, *what)
                            if step == "max" and not (last and g == 3):
                                maximum(u + 1, batch_next, phase, g + 1, what)
                            if step == "mask":
                                mask_later(b, g, s, what)
                            if (step, s) == ("sums", 1) and not (first and g == 0):
                                check_reciprocal(u - 1)
                            if (step, g, s) == ("sums", 1, 0) and not last:
                                layernorm_apply(b + 1)
                            if step == "side":
                                aside(b, g, s, first, last)
            dve.wait_ge(res_in, B * (T * DMA))
            for t in range(T):
                dve.tensor_tensor(res[:, t, :], res[:, t, :], bo_all[:, :], ALU.add).then_inc(res_ready, 1)
            check_reciprocal(B * G - 1)
            correct(B * G - 1, G - 1)
            for t in range(T):
                k = len(of_batch[B - 1]) + 1 + t
                evacuate("o", t, last_banks[t], work_before(B - 1) + k, None, B - 1)

        @block.tensor
        def _(pe):
            def project(to, pairs, part):
                parts_ = range(PARTS) if part is None else (part,)
                size = len(pairs) // PARTS
                for n, (lhs, rhs) in enumerate(pairs):
                    if n // size in parts_:
                        mm = pe.matmul(to[:, :], lhs, rhs, start=(n == 0), stop=(n == len(pairs) - 1))
                if parts_[-1] == PARTS - 1:
                    mm.then_inc(work_full, 1)

            def do_work(kind, nth, bank_, part=None):
                if kind in "hbm" and part:
                    return
                cols = slice(nth * P, (nth + 1) * P)
                if kind in "qk":
                    hi, lo = w_hi[kind], w_lo[kind]
                    project(bank_, [pair for c in range(C) for pair in
                                    ((hi[:, c, cols], h_hi[:, c, :]), (hi[:, c, cols], h_lo[:, c, :]),
                                     (lo[:, c, cols], h_hi[:, c, :]))], part)
                if kind in "vw":
                    if kind == "v":
                        cols = slice((nth + 2) * P, (nth + 3) * P)
                    project(bank_, [pair for c in range(C) for pair in
                                    ((h_hi[:, c, cols], w_hi["v"][:, c, :]), (h_hi[:, c, cols], w_lo["v"][:, c, :]),
                                     (h_lo[:, c, cols], w_hi["v"][:, c, :]))], part)
                if kind == "o":
                    project(bank_, [pair for c in range(C) for pair in
                                    ((attn_hi[:, c, cols], w_hi["o"][:, c, :]), (attn_hi[:, c, cols], w_lo["o"][:, c, :]),
                                     (attn_lo[:, c, cols], w_hi["o"][:, c, :]))], part)
                if kind == "h":
                    for c in range(C):
                        mm = pe.transpose(bank_[:, c * P:(c + 1) * P], x_sb[:, nth, c * P:(c + 1) * P], identf[:, :])
                    mm.then_inc(work_full, 1)
                if kind == "b":
                    tile = bank_[:, 0:S // 2].bitcast(BF16)
                    for t in range(T):
                        mm = pe.transpose(tile[:, t * P:(t + 1) * P], mask_q[:, t, cols], identb[:, :])
                    mm.then_inc(work_full, 1)
                if kind == "m":
                    pe.transpose(bank_[0:MAXIMA, 0:P], top[:, :], identf[:, :]).then_inc(work_full, 1)

            def output_rows(t, to, chunks):
                rows = slice(t * P, (t + 1) * P)
                for c in chunks:
                    pairs = ((attn_hi[:, c, rows], w_hi["o"][:, c, :]), (attn_hi[:, c, rows], w_lo["o"][:, c, :]),
                             (attn_lo[:, c, rows], w_hi["o"][:, c, :]))
                    for n, (lhs, rhs) in enumerate(pairs):
                        mm = pe.matmul(to[:, :], lhs, rhs, start=(c == 0 and n == 0), stop=(c == C - 1 and n == 2))
                return mm

            def maximum(u, phase, g, n):
                slot = stack_slot(phase, g)
                if n == 0:
                    pe.wait_ge(stack_in, (u + 1) * (STACK_DMAS * DMA))
                wait(pe, max_done, u * MAXIMA + (n + 1 - MAX_BANKS))
                t, j = n // HG, n % HG
                pe.matmul(max_bank_of(phase, g, n)[:, :], q_stack[0:3 * DH, slot, j, t * P:(t + 1) * P],
                          k_stack[0:3 * DH, slot, j, :], start=True, stop=True).then_inc(max_full, 1)

            def score(b, g, s, j, slot):
                u = b * G + g
                if j == 0 and s == 0:
                    pe.wait_ge(rows_in, (u + 1) * (2 * DMA))
                if j == 0 and g == 0:
                    pe.wait_ge(mask_k_ready, b * T + (s + 1))
                wait(pe, exp_done, u * SCORES + (s * HG + j - 1))
                to = score_bank[j % 2]
                if j not in MASKED_LATER[s]:
                    pe.matmul(to[:, :], identb[:, :], mask_k[:, s, :], start=True, stop=False)
                pe.matmul(to[:, :], k_stack[0:3 * DH + 2, slot, j, s * P:(s + 1) * P],
                          q_stack[0:3 * DH + 2, slot, j, :], start=(j in MASKED_LATER[s]), stop=True).then_inc(score_full, 1)

            def values(b, g, s):
                u = b * G + g
                pe.wait_ge(exp_done, u * SCORES + (s * HG + HG))
                pe.wait_ge(later_masked, later_count(u, s, MASKED_LATER[s][-1]))
                if g == 0:
                    pe.wait_ge(v_ready, b * T + (s + 1))
                if s == 0:
                    wait(pe, value_copied, u)
                for j in range(HG):
                    h = g * HG + j
                    mm = pe.matmul(value_bank[DH * j:DH * (j + 1), :], v_sb[:, s, h * DH:(h + 1) * DH],
                                   probs[:, s % 2, j, :], start=(s == 0), stop=(s == T - 1))
                mm.then_inc(value_done, 1)

            def sums(u, to):
                pe.wait_ge(add_done, u * ADDS + ADDS)
                for j in range(HG):
                    mm = pe.matmul(to[DH * j:DH * (j + 1), :], ones[:, :], prob_sum[:, j, :],
                                   start=True, stop=True)
                mm.then_inc(work_full, 1)

            emptied = {"v": v_ready, "w": v_ready, "b": mask_k_ready, "o": out_ready, "d": sum_copied}

            def wait_bank(b, k):
                items = items_of(b)
                if k < 2:
                    pe.wait_ge(mask_k_ready, b * T + (T - 1 + k))
                    return
                _, _, kind, nth = items[k - 2]
                if kind == "d":
                    pe.wait_ge(sum_copied, b * G + items[k - 2][0])
                    return
                if kind in emptied:
                    before = {"v": b * T + 2, "w": b * T + T, "b": b * T + T, "o": b * T - T}[kind]
                    pe.wait_ge(emptied[kind], before + (nth + 1))
                else:
                    done = sum(it[2] in "hqkm" for it in items[:k - 2]) + 1
                    pe.wait_ge(split_ready, splits_before(b) + done)

            def wait_item(b, g, s, n, kind):
                k, _ = item_number(b, g, s, n)
                wait_bank(b, k)
                u = b * G + g
                if kind == "h":
                    pe.wait_ge(ln_step, b * LN_STEPS + 2 * LN_STEPS)
                if kind == "q" and g == 2:
                    done = max(i for i, it in enumerate(items_of(b)) if it[2] == "h") + 1
                    pe.wait_ge(split_ready, splits_before(b) + sum(it[2] in "hqkm" for it in items_of(b)[:done]))
                if kind == "b":
                    pe.wait_ge(mask_ready, b * T + 2 * T)
                if kind == "m":
                    pe.wait_ge(max_done, u * MAXIMA + 2 * MAXIMA)
                if kind == "o":
                    pe.wait_ge(w_split, 4)
                    pe.wait_ge(attn_ready, b * G)

            def run_item(b, g, s, n, kind, nth, part):
                group = (g + 2) % 4 if kind in "qk" else nth
                do_work(kind, 0 if kind == "m" else group, work_bank(b, g, s, n), part)

            pe.wait_ge(consts, CONSTS)
            seen = {}
            for n, kind in enumerate(PROLOGUE):
                nth = seen.get(kind, 0)
                if n >= 2:
                    prev = PROLOGUE[n - 2]
                    count = sum(k in "hqkm" if prev in "hqkm" else k == prev for k in PROLOGUE[:n - 1])
                    pe.wait_ge(emptied.get(prev, split_ready), count)
                if kind == "h":
                    pe.wait_ge(ln_step, LN_STEPS)
                if kind in "qk":
                    pe.wait_ge(split_ready, T)
                    pe.wait_ge(w_split, 1 if kind == "q" else 2)
                if kind == "b":
                    pe.wait_ge(mask_ready, T)
                if kind == "w":
                    pe.wait_ge(w_split, 3)
                for product in PROLOGUE_MAXIMA.get(n, ()):
                    maximum(0, 0, 0, product)
                if kind == "m":
                    pe.wait_ge(max_done, MAXIMA)
                do_work(kind, 0 if kind == "m" else nth, work[n % 2])
                seen[kind] = nth + 1

            for b, phase in batches(pe):
                first = isinstance(b, int) and b == 0
                last = isinstance(b, int) and b == B - 1
                for g in range(4):
                    u = b * G + g
                    for s in range(4):
                        items = slot_items(b, g, s)
                        for step, what in steps_of(items, s):
                            if step == "score":
                                score(b, g, s, what, stack_slot(phase, g))
                            if step == "part":
                                (n, kind, nth), part = what
                                if part == 0:
                                    wait_item(b, g, s, n, kind)
                                run_item(b, g, s, n, kind, nth, part)
                            if step == "max" and not (last and g == 3):
                                maximum(u + 1, phase, g + 1, what)
                        if s > 0:
                            values(b, g, s - 1)
                        elif not (first and g == 0):
                            values(b if g > 0 else b - 1, (g - 1) % 4, T - 1)
                            wait_bank(b, item_number(b, g, s, items[-1][0])[0])
                            sums(u - 1, work_bank(b, g, s, items[-1][0]))
            values(B - 1, G - 1, T - 1)
            k = len(of_batch[B - 1])
            pe.wait_ge(out_ready, (B - 1) * T)
            sums(B * G - 1, bank_number(B - 1, k))
            pe.wait_ge(max_done, B * G * MAXIMA)
            pe.wait_ge(sum_copied, B * G - 1)
            pe.wait_ge(attn_ready, B * G - 1)
            for t in range(T):
                output_rows(t, last_banks[t], range(C - 1))
            pe.wait_ge(attn_ready, B * G)
            for t in range(T):
                output_rows(t, last_banks[t], (C - 1,)).then_inc(work_full, 1)


_INS = ["x", "adj", "L0_gnn_Wq", "L0_gnn_bq", "L0_gnn_Wk", "L0_gnn_bk", "L0_gnn_Wv", "L0_gnn_bv",
        "L0_gnn_Wo", "L0_gnn_bo"]


def kernel(**inputs):
    import numpy as _np
    import concourse.bacc as _bacc
    from concourse import mybir as _mybir
    from concourse.bass_utils import run_bass_kernel_spmd as _run

    nc = _bacc.Bacc("TRN2", target_bir_lowering=False, num_devices=1, dynamic_dma_scratch_size=1024)
    arrays, args = {}, []
    for name in _INS:
        a = _np.ascontiguousarray(inputs[name])
        arrays[f"in_{name}_dram"] = a
        args.append(nc.dram_tensor(f"in_{name}_dram", a.shape, _mybir.dt.from_np(a.dtype), kind="ExternalInput").ap())
    shape = inputs["x"].shape
    args.append(nc.dram_tensor("out_0_dram", shape, _mybir.dt.float32, kind="ExternalOutput").ap())
    build_kernel(nc, *args)
    r = _run(nc, [arrays], core_ids=[0])
    return r.results[0]["out_0_dram"]
```
